# Optimizing a Trainium2 kernel written in Bass

```python
import numpy as np
import jax
import jax.numpy as jnp

def _softmax(x, axis=-1):
    return jax.nn.softmax(x, axis=axis)

def _gelu(x):
    return jax.nn.gelu(x, approximate=True)

def _silu(x):
    return jax.nn.silu(x)

def _sigmoid(x):
    return jax.nn.sigmoid(x)

def _layernorm(x, axis=-1, eps=1e-05):
    m = jnp.mean(x, axis=axis, keepdims=True)
    v = jnp.var(x, axis=axis, keepdims=True)
    return (x - m) / jnp.sqrt(v + eps)

def _scatter_add(tgt, idx, src, axis=0):
    return tgt.at[idx].add(src)

def _segment_sum(src, seg, n):
    return jax.ops.segment_sum(src, seg, n)
kernel_name = 'mk_pixart_resid_d1_seqx_r4_8a3e2f'

def setup_inputs(seed: int=0):
    np.random.seed(seed)
    _w = jnp.asarray

    def _rec_inputs():
        import jax
        import jax.numpy as jnp
        _rk = jax.random.key(seed)
        x = -0.0002928 + 1 * jax.random.normal(jax.random.fold_in(_rk, 1), (8, 256, 512), jnp.float32)
        _lenS = 256 - jax.random.randint(jax.random.fold_in(_rk, 7), (8,), 0, max(1, 256 // 4) + 1, jnp.int32)
        _lenS2 = 256 - jax.random.randint(jax.random.fold_in(_rk, 8), (8,), 0, max(1, 256 // 4) + 1, jnp.int32)
        _ctx_2048P = jax.random.normal(jax.random.fold_in(_rk, 11), (8, 16, 512), jnp.float32)
        _ctx_2048c = jax.random.dirichlet(jax.random.fold_in(_rk, 511), 0.3 * jnp.ones((16,), jnp.float32), (8, 256))
        _ctx_2048t = jnp.einsum('bsk,bkd->bsd', _ctx_2048c, _ctx_2048P)
        _ctx_2048t = _ctx_2048t * jax.lax.rsqrt(jnp.mean(jnp.square(_ctx_2048t)) + 1e-12) * 0.953939
        ctx_2048 = -1.39393e-06 + 0.999914 * (_ctx_2048t + 0.3 * jax.random.normal(jax.random.fold_in(_rk, 611), (8, 256, 512), jnp.float32))
        itok_B_779_1933 = jax.random.randint(jax.random.fold_in(_rk, 12), (8,), 779, 1934, jnp.int32)
        return (x, ctx_2048, itok_B_779_1933)
    x, ctx_2048, itok_B_779_1933 = _rec_inputs()

    def _L0_xcond_setup():
        import jax, jax.numpy as jnp
        import numpy as np
        NUM_HEADS = 8
        HEAD_DIM = 64
        AVG_K_LENGTH = 20
        SCALE = 1.0 / (HEAD_DIM ** 0.5 * float(np.log(AVG_K_LENGTH)))
        key = jax.random.key(seed)
        k1, k2, k3, k4 = jax.random.split(key, 4)
        B, HD, LQ, LK = (4, NUM_HEADS * HEAD_DIM, 512, 512)
        q = jax.random.normal(k1, (B, HD, LQ), dtype=jnp.float32)
        k = jax.random.normal(k2, (B, HD, LK), dtype=jnp.float32)
        v = jax.random.normal(k3, (B, HD, LK), dtype=jnp.float32)
        k_length = jax.random.randint(k4, (B,), 128, LK + 1, dtype=jnp.int32)
        return {'q': q, 'k': k, 'v': v, 'k_length': k_length}
    _L0_xcond_all = _L0_xcond_setup()
    _L0_xcond_in = {k: v for k, v in _L0_xcond_all.items() if k in ()}
    del _L0_xcond_all

    def _L0_ffn_setup():
        import jax, jax.numpy as jnp
        import numpy as np
        EPS = 1e-06
        TILES_PER_CLUSTER = 8

        @jax.custom_vjp
        def ste_sign(w):
            return jnp.sign(w)

        def _ste_fwd(w):
            return (jnp.sign(w), None)

        def _ste_bwd(_, g):
            return (g,)
        ste_sign.defvjp(_ste_fwd, _ste_bwd)

        def rmsnorm(x, w):
            var = jnp.mean(x * x, axis=-1, keepdims=True)
            return x * jax.lax.rsqrt(var + EPS) * w
        key = jax.random.key(seed)
        k = jax.random.split(key, 3)
        B, S, D = (4, 512, 512)
        T, H = (64, 128)
        return {'x': jax.random.normal(k[0], (B, S, D), dtype=jnp.float32), 'up_w': jax.random.normal(k[1], (T, H, D), dtype=jnp.float32) * 0.02, 'down_w': jax.random.normal(k[2], (T, D, H), dtype=jnp.float32) * 0.02, 'up_scale': jnp.ones((T, H), dtype=jnp.float32), 'down_scale': jnp.ones((T, D), dtype=jnp.float32), 'output_scale': jnp.ones((T,), dtype=jnp.float32), 'norm_weight': jnp.ones((D,), dtype=jnp.float32)}
    _L0_ffn_all = _L0_ffn_setup()
    _L0_ffn_in = {k: v for k, v in _L0_ffn_all.items() if k in ('up_w', 'down_w', 'up_scale', 'down_scale', 'output_scale', 'norm_weight')}
    del _L0_ffn_all
    return {'x': x, 'ctx_2048': ctx_2048, 'itok_B_779_1933': itok_B_779_1933, 'L0_ffn_up_w': _L0_ffn_in['up_w'], 'L0_ffn_down_w': _L0_ffn_in['down_w'], 'L0_ffn_up_scale': _L0_ffn_in['up_scale'], 'L0_ffn_down_scale': _L0_ffn_in['down_scale'], 'L0_ffn_output_scale': _L0_ffn_in['output_scale'], 'L0_ffn_norm_weight': _L0_ffn_in['norm_weight']}

def reference(x, ctx_2048, itok_B_779_1933, L0_ffn_up_w, L0_ffn_down_w, L0_ffn_up_scale, L0_ffn_down_scale, L0_ffn_output_scale, L0_ffn_norm_weight):
    import jax
    import jax.numpy as jnp

    def _L0_xcond_ref(q, k, v, k_length):
        import jax, jax.numpy as jnp
        import numpy as np
        NUM_HEADS = 8
        HEAD_DIM = 64
        AVG_K_LENGTH = 20
        SCALE = 1.0 / (HEAD_DIM ** 0.5 * float(np.log(AVG_K_LENGTH)))
        b, hd, lq = q.shape
        lk = k.shape[-1]
        d = hd // NUM_HEADS
        qh = q.reshape(b, NUM_HEADS, d, lq)
        kh = k.reshape(b, NUM_HEADS, d, lk)
        vh = v.reshape(b, NUM_HEADS, d, lk)
        s = SCALE * jnp.log(k_length.astype(jnp.float32))[:, None, None, None]
        attn = jnp.einsum('bhdq,bhdk->bhqk', qh, kh)
        attn = jax.nn.softmax(s * attn, axis=-1)
        out = jnp.einsum('bhqk,bhdk->bhdq', attn, vh)
        return out.reshape(b, hd, lq)

    def _L0_ffn_ref(x, up_w, down_w, up_scale, down_scale, output_scale, norm_weight):
        import jax, jax.numpy as jnp
        import numpy as np
        EPS = 1e-06
        TILES_PER_CLUSTER = 8

        @jax.custom_vjp
        def ste_sign(w):
            return jnp.sign(w)

        def _ste_fwd(w):
            return (jnp.sign(w), None)

        def _ste_bwd(_, g):
            return (g,)
        ste_sign.defvjp(_ste_fwd, _ste_bwd)

        def rmsnorm(x, w):
            var = jnp.mean(x * x, axis=-1, keepdims=True)
            return x * jax.lax.rsqrt(var + EPS) * w
        B, S, D = x.shape
        T, H, _ = up_w.shape
        TPC = TILES_PER_CLUSTER
        C = T // TPC
        xf = x.reshape(-1, D)
        xn = rmsnorm(xf, norm_weight)
        tile_sig = jax.lax.stop_gradient(jnp.sign(jnp.sum(jnp.sign(up_w), axis=1)))
        cluster_sig = jnp.sign(tile_sig.reshape(C, TPC, D).mean(axis=1))
        cluster_scores = xn @ cluster_sig.T
        cluster_idx = jnp.argmax(cluster_scores, -1)
        sigs_by_cluster = tile_sig.reshape(C, TPC, D)
        tok_sigs = sigs_by_cluster[cluster_idx]
        local_scores = jnp.einsum('nd,ntd->nt', xn, tok_sigs)
        tile_idx = cluster_idx * TPC + jnp.argmax(local_scores, -1)
        up_sign = ste_sign(up_w)
        down_sign = ste_sign(down_w)
        hidden = xn @ up_sign.reshape(T * H, D).T
        hidden = hidden.reshape(-1, T, H) * up_scale
        hidden = jax.nn.relu(hidden)
        onehot = jax.nn.one_hot(tile_idx, T, dtype=hidden.dtype)
        hidden = (hidden * onehot[:, :, None]).reshape(-1, T * H)
        w_down = jnp.transpose(down_sign, (1, 0, 2)).reshape(D, T * H)
        out = hidden @ w_down.T
        out = out * down_scale[tile_idx] * output_scale[tile_idx][:, None]
        out = xf + out
        return out.reshape(B, S, D)
    x = x + _L0_xcond_ref(_layernorm(x, axis=-1), ctx_2048, ctx_2048, itok_B_779_1933)
    x = x + _L0_ffn_ref(_layernorm(x, axis=-1), L0_ffn_up_w, L0_ffn_down_w, L0_ffn_up_scale, L0_ffn_down_scale, L0_ffn_output_scale, L0_ffn_norm_weight)
    return x

_drawn_inputs = setup_inputs


def setup_inputs(seed=0):
    import zlib

    import numpy as np

    out = dict(_drawn_inputs(seed))
    spreads = {'L0_ffn_up_scale': (1.0, 0.2),
     'L0_ffn_down_scale': (1.0, 0.2),
     'L0_ffn_output_scale': (1.0, 0.2),
     'L0_ffn_norm_weight': (1.0, 0.2)}
    factors = {}
    for name, (base, spread) in spreads.items():
        noise = np.random.default_rng([zlib.crc32(name.encode()), seed]).standard_normal(out[name].shape)
        drawn = base * np.exp(spread * noise) if base else spread * noise
        out[name] = jnp.asarray(drawn.astype(out[name].dtype))
    for name, factor in factors.items():
        out[name] = (out[name] * factor).astype(out[name].dtype)
    return out
```

```python
import math
from contextlib import ExitStack

import concourse.bass as bass
from concourse import mybir

F32 = mybir.dt.float32
F16 = mybir.dt.float16
BF16 = mybir.dt.bfloat16
I32 = mybir.dt.int32
U32 = mybir.dt.uint32
ALU = mybir.AluOpType
ACT = mybir.ActivationFunctionType
AX = mybir.AxisListType
ABSMAX = bass.bass_isa.ReduceOp.absmax

P = 128
B, C, L = 8, 256, 512
HD = 32
HEADS = B * C // HD
GROUPS = B * C // P
GH = P // HD
KC = L // P
EXPERTS, HID = 64, 128
CLUSTERS = 8
BLK = 32
BLOCKS = 128
TOKENS = GROUPS * P
TILES = BLOCKS * BLK // P
TB = P // BLK
CH = 1024
NUP = EXPERTS * HID * KC // CH
ATT_SCALE = 1.0 / (64 ** 0.5 * math.log(20))
LN_EPS, RMS_EPS = 1e-5, 1e-6
ARENA = 19800
EXPO = 0x7F800000
Q_SCALE = 8.0
K_SCALE = 4096.0
X_SCALE = 512.0
H_SCALE = 16.0
LN1_STEPS, LN2_STEPS = 5, 13
YROW = L + 4

C_ID, C_TRI, C_ROWP, C_SELP = 0, 128, 256, 384
C_E64, C_CL64, C_ONES, C_A32, C_SELA, C_TOK, C_P, C_CL8, C_END = 512, 576, 640, 768, 800, 832, 848, 849, 857


def constants():
    import numpy as np

    c = np.zeros((P, C_END), np.float32)
    p, r = np.arange(P)[:, None], np.arange(P)[None, :]
    c[:, C_ID:C_ID + P] = p == r
    c[:, C_TRI:C_TRI + P] = p < r
    c[:, C_ROWP:C_ROWP + P] = r
    c[:, C_SELP:C_SELP + P] = p % TB == r // BLK
    c[:, C_E64:C_E64 + EXPERTS] = np.arange(EXPERTS)
    c[:, C_CL64:C_CL64 + EXPERTS] = np.arange(EXPERTS) // CLUSTERS
    c[:, C_ONES:C_ONES + P] = 1
    c[:, C_A32:C_A32 + TILES] = np.arange(TILES)
    c[:, C_SELA:C_SELA + TILES] = p // TB == np.arange(TILES)[None, :]
    c[:, C_TOK:C_TOK + GROUPS] = p + P * np.arange(GROUPS)[None, :] + 1
    c[:, C_P:C_P + 1] = p
    c[:, C_CL8:C_CL8 + CLUSTERS] = np.arange(CLUSTERS)
    return c


def build(nc, x, ctx_k, ctx_v, klen, up_h, dn_h, us_h, ds_h, os_h, w_h, cst_h, out,
          split_d, ytab, sctab):
    stack = ExitStack()
    with stack:
        def sb(name, shape, dt):
            return stack.enter_context(nc.sbuf_tensor(name, shape, dt))

        def sem(name):
            return stack.enter_context(nc.semaphore(name))

        w_up = sb("w_up", [P, KC, EXPERTS, HID], BF16)
        w_dn = sb("w_dn", [P, EXPERTS, L], BF16)
        ident16 = sb("ident16", [P, P], F16)
        sums_h = sb("sums_h", [P, KC * EXPERTS], F32)
        expscale = sb("expscale", [P, GROUPS], F32)
        small = sb("small", [P, 4], F32)
        us = sb("us", [P, HID], F32)
        wn = sb("wn", [P, KC], F32)

        arena = sb("arena", [P, ARENA], F32)
        used = [0, 0]

        def carve(phase, words):
            a = used[phase]
            used[phase] += words
            assert used[phase] <= ARENA, used
            return arena[:, a:a + words]

        stage = carve(0, 2 * CH).rearrange("p (s n) -> p s n", s=2)
        pt = carve(0, 2 * KC * L).rearrange("p (s c q) -> p s c q", s=2, c=KC)
        qst = carve(0, 2 * GH * L // 2).bitcast(F16).rearrange("p (g j q) -> p g j q", g=2, j=GH)
        kst = carve(0, 2 * GH * L // 2).bitcast(F16).rearrange("p (g j q) -> p g j q", g=2, j=GH)
        vt = carve(0, 2 * KC * 2 * 7 * HD).rearrange("p (g c k n) -> p g c k n", g=2, c=KC, k=2)
        xin = carve(0, L)
        kin = carve(0, L)
        parts = carve(0, 4 * L // 2).bitcast(F16).rearrange("p (s q) -> p s q", s=4)
        xres = carve(0, 2 * L).rearrange("p (s q) -> p s q", s=2)
        att = carve(0, 2 * L).rearrange("p (s q) -> p s q", s=2)
        rden = carve(0, 2 * L).rearrange("p (s q) -> p s q", s=2)
        ident_in = rden[:, 0, 0:P]
        ytile = carve(0, YROW)
        mx = sb("mx", [P, 2, KC], F32)
        mhl = sb("mhl", [P, 2, KC, 2], F16)
        stat = sb("stat", [P, 6], F32)
        mv = sb("mv", [P, 2], F32)
        stat2 = sb("stat2", [P, 6], F32)
        mv2 = sb("mv2", [P, 2], F32)
        sml = sb("sml", [P, 16], F32)
        sm2 = sb("sm2", [P, 16], F32)
        kpow = sb("kpow", [P, 4], F32)
        halves = sb("halves", [P, 2], F32)
        lnk = sb("lnk", [P, B], F32)
        klen_i = sb("klen_i", [P, B], I32)

        cst = carve(1, C_END)
        ident = cst[:, C_ID:C_ID + P]
        rows = carve(1, 4 * YROW).rearrange("p (s n) -> p s n", s=4)
        sigw = carve(1, KC * (EXPERTS + CLUSTERS)).rearrange("p (c e) -> p c e", c=KC)
        csum = carve(1, KC * CLUSTERS).rearrange("p (c e) -> p c e", c=KC)
        ds_sb = carve(1, L)
        os_sb = carve(1, 1)
        scale_sb = carve(1, L)
        mags = carve(1, 4)
        powers = carve(1, 6)
        xt = carve(1, 2 * L).rearrange("p (s c n) -> p s c n", s=2, c=KC)
        score = carve(1, GROUPS * (EXPERTS + CLUSTERS)).rearrange("p (g e) -> p g e", g=GROUPS)
        ckey = carve(1, GROUPS * CLUSTERS).rearrange("p (g e) -> p g e", g=GROUPS)
        before = carve(1, GROUPS * EXPERTS).rearrange("p (g e) -> p g e", g=GROUPS)
        onehot = carve(1, GROUPS * EXPERTS // 2).bitcast(F16).rearrange("p (g e) -> p g e", g=GROUPS)
        pick = [carve(1, GROUPS) for _ in range(6)]
        counts = carve(1, P)
        counts_i = carve(1, P).bitcast(I32)
        nblk = carve(1, P // 2).bitcast(F16)
        ends = carve(1, P)
        ended = carve(1, P // 2).bitcast(F16)
        slot_i = carve(1, 3 * GROUPS).bitcast(I32).rearrange("p (k g) -> p k g", k=3)
        slot_p = carve(1, GROUPS * P // 2).bitcast(F16).rearrange("p (g n) -> p g n", g=GROUPS)
        slot_a = carve(1, GROUPS * TILES // 2).bitcast(F16).rearrange("p (g n) -> p g n", g=GROUPS)
        tri16 = carve(1, P // 2).bitcast(F16)
        ones16 = carve(1, P // 2).bitcast(F16)
        absent = carve(1, TILES)
        token_of = carve(1, TILES).bitcast(I32)
        expert_of = carve(1, BLOCKS).bitcast(I32)
        gidx = carve(1, 4).bitcast(I32)
        sidx = carve(1, 4).bitcast(I32)
        xhl = carve(1, 2 * L).bitcast(F16).rearrange("p (s h c n) -> p s h c n", s=2, h=2, c=KC)
        hid = carve(1, 2 * P).rearrange("p (s n) -> p s n", s=2)
        DIAG = TB * (P + BLK)
        hz = carve(1, 2 * DIAG).bitcast(F16).rearrange("p (s h n) -> p s h n", s=2, h=2)
        scl = carve(1, 2 * L).rearrange("p (s n) -> p s n", s=2)
        base = carve(1, 2 * L).rearrange("p (s n) -> p s n", s=2)
        res = carve(1, 4 * L).rearrange("p (s n) -> p s n", s=4)
        work = [res.rearrange("p s n -> p (s n)")[:, k * GROUPS * EXPERTS:(k + 1) * GROUPS * EXPERTS]
                .rearrange("p (g e) -> p g e", g=GROUPS) for k in range(2)]
        live = carve(1, P)
        us_of = carve(1, BLOCKS)

        sq_ps = stack.enter_context(nc.psum_tensor("sq_ps", [P, 2, L], F32))
        pv_ps = stack.enter_context(nc.psum_tensor("pv_ps", [P, L], F32))
        mt_ps = stack.enter_context(nc.psum_tensor("mt_ps", [P, L], F32))
        st_ps = stack.enter_context(nc.psum_tensor("st_ps", [P, 4, L], F32))
        banks = [sq_ps[:, 0, :], sq_ps[:, 1, :], pv_ps[:, :], mt_ps[:, :]]

        const_in = sem("const_in")
        setup_dve = sem("setup_dve")
        setup_pool = sem("setup_pool")
        lnk_ready = sem("lnk_ready")
        consts_ready = sem("consts_ready")
        sctab_out = sem("sctab_out")
        xk_in = sem("xk_in")
        v_in = sem("v_in")
        xres_in = sem("xres_in")
        stats_ready = sem("stats_ready")
        moments_ready = sem("moments_ready")
        kmax_ready = sem("kmax_ready")
        kmax_all = sem("kmax_all")
        ln1_step = sem("ln1_step")
        kpow_step = sem("kpow_step")
        q_ready = sem("q_ready")
        hi_ready = sem("hi_ready")
        parts_ready = sem("parts_ready")
        split_out = sem("split_out")
        stack_in = sem("stack_in")
        sq_done = sem("sq_done")
        max_done = sem("max_done")
        mhi_done = sem("mhi_done")
        mneg_done = sem("mneg_done")
        mrow_done = sem("mrow_done")
        mrow_copied = sem("mrow_copied")
        st_done = sem("st_done")
        exp_done = sem("exp_done")
        pv_done = sem("pv_done")
        rden_done = sem("rden_done")
        att_evac = sem("att_evac")
        ratio_done = sem("ratio_done")
        x2_done = sem("x2_done")
        stats2_ready = sem("stats2_ready")
        moments2_ready = sem("moments2_ready")
        ln2_step = sem("ln2_step")
        y_done = sem("y_done")
        y_out = sem("y_out")
        w_in = [sem("w_in0"), sem("w_in1")]
        sign_done = sem("sign_done")
        sums_done = sem("sums_done")

        scale_in = sem("scale_in")
        mags_ready = sem("mags_ready")
        mags_all = sem("mags_all")
        ffn_step = sem("ffn_step")
        sig_tiles = sem("sig_tiles")
        csum_ready = sem("csum_ready")
        sig_clusters = sem("sig_clusters")
        sig_ready = sem("sig_ready")
        sctab_ready = sem("sctab_ready")
        row_in = [sem("row_in0"), sem("row_in1")]
        tok_t = sem("tok_t")
        xt_ready = sem("xt_ready")
        score_done = sem("score_done")
        score_copied = sem("score_copied")
        onehot_ready = sem("onehot_ready")
        rank_done = sem("rank_done")
        count_done = sem("count_done")
        nblk_ready = sem("nblk_ready")
        start_done = sem("start_done")
        ended_ready = sem("ended_ready")
        expert_done = sem("expert_done")
        expert_ready = sem("expert_ready")
        slots_ready = sem("slots_ready")
        list_done = sem("list_done")
        list_ready = sem("list_ready")
        clean = sem("clean")
        gidx_ready = sem("gidx_ready")
        sidx_ready = sem("sidx_ready")
        gathered = [sem(f"gathered{k}") for k in range(4)]
        slot_t = sem("slot_t")
        xhi_ready = sem("xhi_ready")
        xlo_ready = sem("xlo_ready")
        up_done = sem("up_done")
        live_ready = sem("live_ready")
        us_done = sem("us_done")
        hid_ready = sem("hid_ready")
        hhi_ready = sem("hhi_ready")
        hlo_ready = sem("hlo_ready")
        down_done = sem("down_done")
        scl_in = [sem("scl_in0"), sem("scl_in1")]
        base_ready = sem("base_ready")
        prod_ready = sem("prod_ready")
        res_ready = sem("res_ready")
        scattered = [sem(f"scattered{k}") for k in range(4)]
        cst_in = sem("cst_in")

        def wait(eng, s, v):
            if not (isinstance(v, int) and v <= 0):
                eng.wait_ge(s, v)

        class Head:

            def __init__(self, i, jj):
                self.n, self.j, self.slot = 8 * i + jj, jj % GH, jj % 2
                self.g, self.par = 2 * i + jj // GH, jj // GH % 2
                self.pair = 4 * i + jj // 2
                self.exists = not isinstance(i, int) or 0 <= self.n < HEADS

        def settle(eng):
            eng.sem_inc(settled[eng.engine], 1)

        def ok(g):
            return not isinstance(g, int) or 0 <= g < GROUPS

        def bodies(eng, body, last=1):
            body(0)
            with eng.Fori(1, B - last) as i:
                body(i)
            for i in range(B - last, B):
                body(i)

        settled = {e.engine: sem(f"settled{k}") for k, e in enumerate(
            (nc.scalar, nc.vector, nc.gpsimd, nc.sync, nc.tensor))}
        attention = ExitStack()
        block = attention.enter_context(nc.Block())

        @block.sync
        def _(sp):
            sp.dma_start(ident_in, cst_h[:, C_ID:C_ID + P]).then_inc(const_in, 16)
            sp.dma_start(klen_i[:, :], bass.AP(klen.tensor, 0, [[0, P], [1, B]])).then_inc(const_in, 16)
            sp.dma_start(us[0:EXPERTS, :], us_h).then_inc(const_in, 16)
            sp.dma_start(wn[:, :], w_h).then_inc(const_in, 16)

            def load_in(g):
                if not ok(g):
                    return
                wait(sp, parts_ready, 2 * g)
                sp.dma_start(xin, x[bass.ds(g, 1)].rearrange("a p q -> (a p) q")).then_inc(xk_in, 16)
                sp.dma_start(kin, ctx_k[bass.ds(g, 1)].rearrange("a p q -> (a p) q")).then_inc(xk_in, 16)

            def put_parts(g):
                if not ok(g):
                    return
                wait(sp, parts_ready, 2 * (g + 1))
                sp.dma_start(split_d[bass.ds(g, 1)].rearrange("a p s q -> (a p) s q"), parts)\
                    .then_inc(split_out, 16)

            def load_stacks(g, par):
                if not ok(g):
                    return
                counts = [16 * (g + 1), 8 * (g - 1)]
                if not isinstance(g, int):
                    counts = [sp.snap(c) for c in counts]
                wait(sp, split_out, counts[0])
                settle(sp)
                wait(sp, st_done, counts[1])
                src = split_d[bass.ds(g, 1)].rearrange("a (j d) s q -> d (a j) s q", j=GH)
                for r, (sq, sk) in enumerate(((0, 2), (0, 3), (1, 2))):
                    rows = slice(r * HD, (r + 1) * HD)
                    sp.dma_start(qst[rows, par], src[:, :, sq]).then_inc(stack_in, 16)
                    sp.dma_start(kst[rows, par], src[:, :, sk]).then_inc(stack_in, 16)

            def load_v(g, par):
                if not ok(g):
                    return
                wait(sp, pv_done, 4 * (g - 1))
                for e in range(2):
                    sp.dma_start(
                        vt[:, par, :, :, e * 4 * HD:(e * 4 + 1) * HD].rearrange("p c k n -> p (c k) n"),
                        ctx_v[bass.ds(g, 1), e].rearrange("a p c n -> (a p) c n")).then_inc(v_in, 16)

            def load_res(g, par):
                wait(sp, x2_done, g - 1)
                sp.dma_start(xres[:, par], x[bass.ds(g, 1)].rearrange("a p q -> (a p) q"))\
                    .then_inc(xres_in, 16)

            def put_y(g):
                if not ok(g):
                    return
                wait(sp, y_done, g + 1)
                sp.dma_start(ytab[bass.ds(g, 1)].rearrange("a p q -> (a p) q"), ytile)\
                    .then_inc(y_out, 16)

            load_in(0)
            put_parts(0)
            load_in(1)
            load_stacks(0, 0)
            sp.wait_ge(setup_pool, 1)
            load_v(0, 0)
            put_parts(1)
            load_in(2)
            load_stacks(1, 1)

            def body(i):
                for par in range(2):
                    g = 2 * i + par
                    load_res(g, par)
                    load_v(g + 1, 1 - par)
                    put_y(g - 2)
                    put_parts(g + 2)
                    load_in(g + 3)
                    load_stacks(g + 2, par)

            bodies(sp, body, last=2)
            put_y(GROUPS - 2)
            put_y(GROUPS - 1)

        @block.tensor
        def _(pe):
            def scores_q(h, half):
                if not h.exists:
                    return
                if h.j == 0 and half == 0:
                    wait(pe, stack_in, 96 * h.g + 96)
                wait(pe, max_done, 2 * h.n + half)
                for t in range(2):
                    q = (2 * half + t) * P
                    mm = pe.matmul(sq_ps[:, t, :], qst[0:96, h.par, h.j, q:q + P],
                                   kst[0:96, h.par, h.j, :], start=True, stop=True)
                mm.then_inc(sq_done, 1)

            def max_rows(h):
                if not h.exists:
                    return
                wait(pe, mneg_done, h.n + 1)
                wait(pe, mrow_copied, h.n)
                for t in range(KC):
                    mm = pe.matmul(mt_ps[96:98, t * P:(t + 1) * P], mhl[:, h.slot, t, :], ident16[:, :],
                                   start=True, stop=True)
                mm.then_inc(mrow_done, 1)

            def scores_k(h, half):
                wait(pe, mrow_copied, h.n + 1)
                wait(pe, exp_done, 2 * h.n - 1 + half)
                for c in (2 * half, 2 * half + 1):
                    mm = pe.matmul(st_ps[:, c, :], kst[0:98, h.par, h.j, c * P:(c + 1) * P],
                                   qst[0:98, h.par, h.j, :], start=True, stop=True)
                mm.then_inc(st_done, 1)

            def values(h, half):
                if not h.exists:
                    return
                if half == 0 and h.j == 0:
                    wait(pe, v_in, 32 * h.g + 32)
                if half == 0 and h.slot == 0:
                    wait(pe, att_evac, h.pair)
                wait(pe, exp_done, 2 * h.n + 1 + half)
                e = h.slot
                for c in (2 * half, 2 * half + 1):
                    mm = pe.matmul(pv_ps[:, :], vt[:, h.par, c, h.j // 2, 3 * HD * e:3 * HD * e + P],
                                   pt[:, h.slot, c, :], start=(e == 0 and c == 0),
                                   stop=(e == 1 and c == KC - 1))
                if half == 1:
                    mm.then_inc(pv_done, 1)

            pe.wait_ge(consts_ready, 3)
            for off in (0, 1):
                for half in range(2):
                    scores_q(Head(0, off), half)
            max_rows(Head(0, 0))

            def body(i):
                for jj in range(2 * GH):
                    scores_k(Head(i, jj), 0)
                    scores_q(Head(i, jj + 2), 0)
                    values(Head(i, jj - 1), 0)
                    scores_k(Head(i, jj), 1)
                    max_rows(Head(i, jj + 1))
                    scores_q(Head(i, jj + 2), 1)
                    values(Head(i, jj - 1), 1)

            bodies(pe, body)
            values(Head(B - 1, 7), 0)
            values(Head(B - 1, 7), 1)

        @block.scalar
        def _(act):
            def load_w(h):
                if not h.exists:
                    return
                wait(act, sign_done, h.n - 1)
                act.dma_start(stage[:, h.slot], (up_h, dn_h)[h.slot][bass.ds(h.pair, 1)]
                              .rearrange("a p n -> (a p) n")).then_inc(w_in[h.slot], 16)

            load_w(Head(0, 0))
            load_w(Head(0, 1))
            act.wait_ge(setup_dve, 1)
            act.activation(lnk[:, :], lnk[:, :], ACT.Ln).then_inc(lnk_ready, 1)

            def norm_q(g):
                if not ok(g):
                    return
                wait(act, ln1_step, LN1_STEPS * g + LN1_STEPS)
                act.activation(xin, xin, ACT.Identity, bias=sml[:, 3:4], scale=sml[:, 2:3])\
                    .then_inc(q_ready, 1)

            def copy_rows(h):
                if not h.exists:
                    return
                wait(act, mrow_done, h.n + 1)
                act.activation(qst[96:98, h.par, h.j, :], mt_ps[96:98, :], ACT.Copy)\
                    .then_inc(mrow_copied, 1)

            def exps(h, half):
                wait(act, st_done, 2 * h.n + 1 + half)
                wait(act, pv_done, h.n - 1)
                settle(act)
                act.activation(pt[:, h.slot, 2 * half:2 * half + 2, :], st_ps[:, 2 * half:2 * half + 2, :],
                               ACT.Exp, scale=expscale[:, bass.ds(h.g, 1)]).then_inc(exp_done, 1)

            def evacuate(h):
                if not h.exists:
                    return
                rows = slice(64 * (h.j // 2), 64 * (h.j // 2) + 64)
                wait(act, pv_done, h.n + 1)
                if h.j == 1:
                    wait(act, y_done, h.g - 1)
                act.activation(rden[rows, h.par], pv_ps[64:128, :], ACT.Copy)
                act.activation(att[rows, h.par], pv_ps[0:64, :], ACT.Copy).then_inc(att_evac, 1)

            def signs(h):
                wait(act, w_in[h.slot], 16 * h.pair + 16)
                dst = (w_up[:, :, :, :].rearrange("p c e h -> p (c e h)"),
                       w_dn[:, :, :].rearrange("p e n -> p (e n)"))[h.slot]
                act.activation(dst[:, bass.ds(h.pair * CH, CH)], stage[:, h.slot], ACT.Sign)\
                    .then_inc(sign_done, 1)

            def norm_y(g, par):
                if not ok(g):
                    return
                wait(act, ln2_step, LN2_STEPS * g + LN2_STEPS)
                act.activation(ytile[:, 0:L], att[:, par], ACT.Identity, bias=sm2[:, 7:8],
                               scale=sm2[:, 6:7]).then_inc(y_done, 1)

            norm_q(0)
            norm_q(1)
            copy_rows(Head(0, 0))

            def body(i):
                for jj in range(2 * GH):
                    h = Head(i, jj)
                    if h.slot == 1:
                        evacuate(Head(i, jj - 2))
                    exps(h, 0)
                    copy_rows(Head(i, jj + 1))
                    exps(h, 1)
                    signs(h)
                    if h.j == 1:
                        norm_y(h.g - 2, h.par)
                        norm_q(h.g + 2)
                    load_w(Head(i, jj + 2))

            bodies(act, body)
            evacuate(Head(B - 1, 7))
            norm_y(GROUPS - 2, 0)
            norm_y(GROUPS - 1, 1)

        @block.vector
        def _(dve):
            dve.wait_ge(const_in, 64)
            dve.tensor_copy(lnk[:, :], klen_i[:, :]).then_inc(setup_dve, 1)
            dve.tensor_copy(ident16[:, :], ident_in).then_inc(consts_ready, 1)
            dve.memset(kst[96:98, 0, :, :], K_SCALE).then_inc(consts_ready, 1)
            dve.memset(kst[96:98, 1, :, :], K_SCALE).then_inc(consts_ready, 1)
            dve.wait_ge(lnk_ready, 1)
            dve.tensor_scalar(lnk[:, :], lnk[:, :], ATT_SCALE / (Q_SCALE * K_SCALE), None, ALU.mult)\
                .then_inc(setup_dve, 1)

            def prep_stats(g):
                if not ok(g):
                    return
                wait(dve, xk_in, 32 * g + 32)
                dve.bn_stats(stat[:, :], xin).then_inc(stats_ready, 1)
                wait(dve, kpow_step, 4 * g)
                dve.tensor_reduce(small[:, 0:1], kin, AX.X, ALU.max, apply_absolute_value=True)\
                    .then_inc(kmax_ready, 1)
                wait(dve, stats_ready, g + 1)
                wait(dve, q_ready, g)
                settle(dve)
                dve.bn_aggr(mv[:, :], stat[:, :]).then_inc(moments_ready, 1)

            def prep_kpow(g, b):
                if not ok(g):
                    return
                wait(dve, kmax_all, g + 1)
                dve.tensor_scalar(kpow[:, 0:1], small[:, 1:2], 2.0 ** -60, None, ALU.max)\
                    .then_inc(kpow_step, 1)
                wait(dve, kpow_step, 4 * g + 1)
                dve.tensor_scalar(kpow[:, 1:2].bitcast(I32), kpow[:, 0:1].bitcast(I32), EXPO, None,
                                  ALU.bitwise_and).then_inc(kpow_step, 1)
                wait(dve, kpow_step, 4 * g + 2)
                dve.tensor_scalar(kpow[:, 2:3].bitcast(I32), kpow[:, 1:2].bitcast(I32), -1.0,
                                  float(0x7F000000 + (12 << 23)), ALU.mult, ALU.add)\
                    .then_inc(kpow_step, 1)
                wait(dve, setup_dve, 2)
                dve.tensor_tensor(expscale[:, bass.ds(g, 1)], kpow[:, 1:2], lnk[:, bass.ds(b, 1)],
                                  ALU.mult).then_inc(kpow_step, 1)

            def prep_k(g):
                if not ok(g):
                    return
                wait(dve, kpow_step, 4 * g + 3)
                wait(dve, split_out, 16 * g)
                dve.tensor_scalar(parts[:, 2], kin, kpow[:, 2:3], None, ALU.mult).then_inc(hi_ready, 1)
                wait(dve, hi_ready, 2 * g + 1)
                dve.scalar_tensor_tensor(parts[:, 3], kin, kpow[:, 2:3], parts[:, 2], ALU.mult,
                                         ALU.subtract).then_inc(parts_ready, 1)

            def prep_q(g):
                if not ok(g):
                    return
                wait(dve, q_ready, g + 1)
                dve.tensor_copy(parts[:, 0], xin).then_inc(hi_ready, 1)
                wait(dve, hi_ready, 2 * g + 2)
                dve.tensor_tensor(parts[:, 1], xin, parts[:, 0], ALU.subtract).then_inc(parts_ready, 1)

            def maxima(h):
                if not h.exists:
                    return
                wait(dve, mneg_done, h.n - 1)
                for half in range(2):
                    wait(dve, sq_done, 2 * h.n + half + 1)
                    dve.tensor_reduce(mx[:, h.slot, 2 * half:2 * half + 2], sq_ps[:, :, :], AX.X,
                                      ALU.max, negate=True).then_inc(max_done, 1)
                wait(dve, max_done, 2 * h.n + 2)
                wait(dve, mrow_done, h.n - 1)
                dve.tensor_scalar(mhl[:, h.slot, :, 0], mx[:, h.slot, :], 1.0 / K_SCALE, None, ALU.mult)\
                    .then_inc(mhi_done, 1)
                wait(dve, mhi_done, h.n + 1)
                dve.scalar_tensor_tensor(mhl[:, h.slot, :, 1], mx[:, h.slot, :], 1.0 / K_SCALE,
                                         mhl[:, h.slot, :, 0], ALU.mult, ALU.subtract)\
                    .then_inc(mneg_done, 1)

            def invert(g, par, q):
                if not ok(g):
                    return
                if q == 0:
                    wait(dve, att_evac, 2 * g + 2)
                    settle(dve)
                cols = slice(q * P, (q + 1) * P)
                dve.reciprocal(rden[:, par, cols], rden[:, par, cols]).then_inc(rden_done, 1)

            def stats2(g, par):
                if not ok(g):
                    return
                wait(dve, x2_done, g + 1)
                dve.bn_stats(stat2[:, :], att[:, par]).then_inc(stats2_ready, 1)
                wait(dve, stats2_ready, g + 1)
                wait(dve, ln2_step, LN2_STEPS * g)
                settle(dve)
                dve.bn_aggr(mv2[:, :], stat2[:, :]).then_inc(moments2_ready, 1)

            def sum_signs(k):
                wait(dve, sign_done, 2 * k + 1)
                src = w_up[:, :, :, :].rearrange("p c e h -> p (c e h)")
                dve.tensor_reduce(sums_h[:, bass.ds(8 * k, 8)],
                                  src[:, bass.ds(k * CH, CH)].rearrange("p (e h) -> p e h", h=HID),
                                  AX.X, ALU.add).then_inc(sums_done, 1)

            for g in range(2):
                prep_stats(g)
                prep_kpow(g, 0)
                prep_k(g)
                prep_q(g)
            maxima(Head(0, 0))
            maxima(Head(0, 1))

            def body(i):
                for jj in range(2 * GH):
                    h = Head(i, jj)
                    maxima(Head(i, jj + 2))
                    if h.j == 0:
                        prep_stats(h.g + 2)
                    if h.j in (1, 2):
                        for q in (0, 1):
                            invert(h.g - 1, 1 - h.par, 2 * (h.j - 1) + q)
                    if h.j == 1:
                        prep_kpow(h.g + 2, i + 1)
                        prep_k(h.g + 2)
                    if h.j == 2:
                        prep_q(h.g + 2)
                    if h.j == 3:
                        stats2(h.g - 1, 1 - h.par)
                    if h.slot == 1:
                        sum_signs(h.pair)

            bodies(dve, body)
            for q in range(KC):
                invert(GROUPS - 1, 1, q)
            stats2(GROUPS - 1, 1)

        @block.gpsimd
        def _(pool):
            pool.memset(vt[:, :, :, :, HD:2 * HD], 0.0)
            pool.memset(vt[:, :, :, :, 3 * HD:4 * HD], 0.0)
            pool.memset(vt[:, :, :, :, 5 * HD:6 * HD], 0.0)
            pool.memset(vt[:, :, :, :, 2 * HD:3 * HD], 1.0)
            pool.memset(halves[:, 0:1], -0.5)
            pool.memset(halves[:, 1:2], 0.5)
            pool.memset(ytile[:, L + 2:YROW], 0.0)
            pool.memset(vt[:, :, :, :, 6 * HD:7 * HD], 1.0).then_inc(setup_pool, 1)
            pool.wait_ge(setup_pool, 1)

            def ln1(g):
                if not ok(g):
                    return
                s = LN1_STEPS * g
                wait(pool, kmax_ready, g + 1)
                settle(pool)
                pool.partition_all_reduce(small[:, 1:2], small[:, 0:1], P, ABSMAX).then_inc(kmax_all, 1)
                wait(pool, moments_ready, g + 1)
                settle(pool)
                pool.tensor_scalar(sml[:, 0:1], mv[:, 1:2], LN_EPS, None, ALU.add).then_inc(ln1_step, 1)
                wait(pool, ln1_step, s + 1)
                pool.tensor_tensor(sml[:, 1:2], sml[:, 0:1], halves[:, 0:1], ALU.pow).then_inc(ln1_step, 1)
                wait(pool, ln1_step, s + 2)
                settle(pool)
                pool.tensor_scalar(sml[:, 2:3], sml[:, 1:2], Q_SCALE, None, ALU.mult).then_inc(ln1_step, 1)
                wait(pool, ln1_step, s + 3)
                pool.tensor_tensor(sml[:, 4:5], mv[:, 0:1], sml[:, 2:3], ALU.mult).then_inc(ln1_step, 1)
                wait(pool, ln1_step, s + 4)
                settle(pool)
                pool.tensor_scalar(sml[:, 3:4], sml[:, 4:5], -1.0, None, ALU.mult).then_inc(ln1_step, 1)

            def residual(g, par):
                if not ok(g):
                    return
                wait(pool, rden_done, KC * g + KC)
                pool.tensor_tensor(att[:, par], att[:, par], rden[:, par], ALU.mult).then_inc(ratio_done, 1)
                wait(pool, ratio_done, g + 1)
                wait(pool, xres_in, 16 * g + 16)
                pool.tensor_tensor(att[:, par], att[:, par], xres[:, par], ALU.add).then_inc(x2_done, 1)

            def ln2(g):
                if not ok(g):
                    return
                steps = [0]

                def step(ins):
                    steps[0] += 1
                    ins.then_inc(ln2_step, 1)
                    wait(pool, ln2_step, LN2_STEPS * g + steps[0])
                    settle(pool)

                wait(pool, moments2_ready, g + 1)
                wait(pool, y_done, g)
                settle(pool)
                c = [sm2[:, k:k + 1] for k in range(12)]
                step(pool.tensor_scalar(c[0], mv2[:, 1:2], LN_EPS, None, ALU.add))
                step(pool.tensor_tensor(c[1], c[0], halves[:, 0:1], ALU.pow))
                step(pool.tensor_tensor(c[2], c[0], halves[:, 1:2], ALU.pow))
                step(pool.tensor_tensor(c[3], c[1], c[1], ALU.mult))
                step(pool.tensor_tensor(c[3], c[3], mv2[:, 1:2], ALU.mult))
                step(pool.tensor_scalar(c[3], c[3], RMS_EPS, None, ALU.add))
                step(pool.tensor_tensor(c[4], c[3], halves[:, 0:1], ALU.pow))
                step(pool.tensor_tensor(c[5], c[3], halves[:, 1:2], ALU.pow))
                step(pool.tensor_tensor(c[6], c[1], c[4], ALU.mult))
                step(pool.tensor_tensor(c[8], c[6], mv2[:, 0:1], ALU.mult))
                step(pool.tensor_scalar(c[7], c[8], -1.0, None, ALU.mult))
                wait(pool, y_out, 16 * g)
                settle(pool)
                step(pool.tensor_scalar(ytile[:, L:L + 1], c[2], 1.0, c[5], ALU.add, ALU.mult))
                step(pool.tensor_copy(ytile[:, L + 1:L + 2], mv2[:, 0:1]))

            ln1(0)
            ln1(1)

            def body(i):
                for par in range(2):
                    g = 2 * i + par
                    ln1(g + 2)
                    residual(g - 1, 1 - par)
                    ln2(g - 1)

            bodies(pool, body)
            residual(GROUPS - 1, 1)
            ln2(GROUPS - 1)

        attention.close()
        block = stack.enter_context(nc.Block())

        def passes(eng, body, n, first=1, last=1):
            for i in range(first):
                body(i)
            with eng.Fori(first, n - last) as i:
                body(i)
            for i in range(n - last, n):
                body(i)

        class Tile:

            def __init__(self, i, jj, count=TILES, per_pass=4):
                self.n, self.par, self.slot = per_pass * i + jj, jj % 2, jj % per_pass
                self.turn = per_pass // 2 * i + jj // 2
                self.slot_turn = i + jj // per_pass
                self.exists = not isinstance(i, int) or 0 <= self.n < count

        def registers(eng, name):
            return [[eng.alloc_register(f"{name}{par}{b}") for b in range(TB)] for par in range(2)]

        def load_experts(eng, regs, tile):
            settle(eng)
            eng.load(regs[tile.par], expert_of[0:1, bass.ds(TB * tile.n, TB)])

        def expert(eng, regs, tile, b):
            return eng.snap(regs[tile.par][b], min_val=0, max_val=EXPERTS - 1)

        @block.sync
        def _(sp):
            sp.dma_start(cst, cst_h).then_inc(cst_in, 16)
            sp.dma_start(ds_sb[0:EXPERTS], ds_h).then_inc(scale_in, 16)
            sp.dma_start(os_sb[0:EXPERTS], os_h).then_inc(scale_in, 16)

            sp_regs = registers(sp, "sp_expert")

            def load_rows(tile):
                if not tile.exists:
                    return
                g, par = tile.n, tile.par
                wait(sp, tok_t, g - 1)
                sp.dma_start(rows[:, par], ytab[bass.ds(g, 1)].rearrange("a p q -> (a p) q"))\
                    .then_inc(row_in[par], 16)

            def load_scales(tile):
                t, par = tile.n, tile.par
                wait(sp, prod_ready, t - 1)
                load_experts(sp, sp_regs, tile)
                for b in range(TB):
                    e = expert(sp, sp_regs, tile, b)
                    sp.dma_start(scl[b * BLK:(b + 1) * BLK, par],
                                 sctab[bass.ds(e, 1), :].broadcast_to([BLK, L])).then_inc(scl_in[par], 16)

            def body_rows(i):
                for par in range(2):
                    load_rows(Tile(i, par, GROUPS, 2))

            def body_scales(i):
                for k in range(4):
                    load_scales(Tile(i, k))

            passes(sp, body_rows, GROUPS // 2)
            sp.wait_ge(sctab_ready, 1)
            sp.dma_start(sctab, scale_sb[0:EXPERTS]).then_inc(sctab_out, 16)
            sp.wait_ge(sctab_out, 16)
            sp.wait_ge(expert_ready, 1)
            passes(sp, body_scales, TILES // 4)

        @block.tensor
        def _(pe):
            t_ps = [st_ps[:, k, :].rearrange("p (c n) -> p c n", c=KC) for k in range(2)]
            h_ps = [st_ps[:, k, 0:P] for k in (2, 3)]
            pe_regs = registers(pe, "pe_expert")

            def turn_rows(tile):
                if not tile.exists:
                    return
                g, par = tile.n, tile.par
                wait(pe, row_in[par], 16 * tile.turn + 16)
                wait(pe, xt_ready, g - 1)
                for c in range(KC):
                    mm = pe.transpose(t_ps[par][:, c, :], rows[:, par, c * P:(c + 1) * P], ident)
                mm.then_inc(tok_t, 1)

            def scores(tile):
                g, par = tile.n, tile.par
                wait(pe, xt_ready, g + 1)
                wait(pe, score_copied, g - 1)
                for c in range(KC):
                    mm = pe.matmul(banks[par][:, 0:EXPERTS + CLUSTERS], xt[:, par, c], sigw[:, c],
                                   start=(c == 0), stop=(c == KC - 1))
                mm.then_inc(score_done, 1)

            def body_scores(i):
                for par in range(2):
                    turn_rows(Tile(i, par + 1, GROUPS, 2))
                    if par == 0 and isinstance(i, int) and i == 0:
                        pe.wait_ge(sig_ready, 1)
                    scores(Tile(i, par, GROUPS, 2))

            pe.wait_ge(cst_in, 16)
            turn_rows(Tile(0, 0, GROUPS, 2))
            passes(pe, body_scores, GROUPS // 2)

            pe.wait_ge(onehot_ready, 1)
            flat = onehot[:, :, :].rearrange("p g e -> p (g e)")
            for g in range(GROUPS):
                mm = pe.matmul(banks[2][0:EXPERTS, 0:P], onehot[:, g, :], ones16,
                               start=(g == 0), stop=(g == GROUPS - 1))
            mm.then_inc(count_done, 1)
            for half in range(2):
                cols = slice(half * L, (half + 1) * L)
                pe.matmul(st_ps[:, half, :], tri16, flat[:, cols], start=True, stop=True)
                mm = pe.matmul(st_ps[:, 2 + half, :], ones16, flat[:, cols], start=True, stop=True)
            mm.then_inc(rank_done, 1)
            pe.wait_ge(nblk_ready, 1)
            pe.matmul(banks[0][:, 0:EXPERTS], nblk[0:EXPERTS], tri16[0:EXPERTS, 0:EXPERTS],
                      start=True, stop=True)
            pe.matmul(banks[1][0:EXPERTS, 0:P], tri16[0:EXPERTS, 0:EXPERTS], nblk[0:EXPERTS],
                      start=True, stop=True).then_inc(start_done, 1)
            pe.wait_ge(ended_ready, 1)
            pe.matmul(banks[3][:, 0:BLOCKS], ones16[0:EXPERTS], ended[0:EXPERTS],
                      start=True, stop=True).then_inc(expert_done, 1)
            pe.wait_ge(live_ready, 1)
            pe.matmul(banks[1][:, 0:BLOCKS], us[0:EXPERTS], live[0:EXPERTS],
                      start=True, stop=True).then_inc(us_done, 1)
            pe.wait_ge(slots_ready, 1)
            for g in range(GROUPS):
                mm = pe.matmul(banks[2][:, 0:TILES], slot_p[:, g], slot_a[:, g],
                               start=(g == 0), stop=(g == GROUPS - 1))
            mm.then_inc(list_done, 1)

            def turn_slots(tile):
                if not tile.exists:
                    return
                t, par = tile.n, tile.par
                wait(pe, gathered[tile.slot], 16 * tile.slot_turn + 16)
                wait(pe, xlo_ready, t - 1)
                for c in range(KC):
                    mm = pe.transpose(t_ps[par][:, c, :], rows[:, tile.slot, c * P:(c + 1) * P], ident)
                mm.then_inc(slot_t, 1)

            def up(tile):
                t, par = tile.n, tile.par
                wait(pe, xlo_ready, t + 1)
                wait(pe, hid_ready, t - 1)
                load_experts(pe, pe_regs, tile)
                for b in range(TB):
                    e = expert(pe, pe_regs, tile, b)
                    cols = slice(b * BLK, (b + 1) * BLK)
                    for c in range(KC):
                        w = w_up[:, c, bass.ds(e, 1), :].rearrange("p a h -> p (a h)")
                        for k in range(2):
                            mm = pe.matmul(h_ps[par][:, cols], w, xhl[:, par, k, c, cols],
                                           start=(c == 0 and k == 0), stop=(c == KC - 1 and k == 1))
                mm.then_inc(up_done, 1)

            def down(tile):
                if not tile.exists:
                    return
                t, par = tile.n, tile.par
                wait(pe, hlo_ready, t + 1)
                wait(pe, prod_ready, t - 1)
                for b in range(TB):
                    e = expert(pe, pe_regs, tile, b)
                    w = w_dn[:, bass.ds(e, 1), :].rearrange("p a n -> p (a n)")
                    for k in range(2):
                        mm = pe.matmul(banks[par], hz[:, par, k, b * P:(b + 1) * P], w,
                                       start=(b == 0 and k == 0), stop=(b == TB - 1 and k == 1))
                mm.then_inc(down_done, 1)

            def body_slots(i):
                for k in range(4):
                    turn_slots(Tile(i, k + 1))
                    up(Tile(i, k))
                    down(Tile(i, k - 1))

            pe.wait_ge(expert_ready, 1)
            turn_slots(Tile(0, 0))
            passes(pe, body_slots, TILES // 4)
            down(Tile(TILES // 4 - 1, 3))

        @block.scalar
        def _(act):
            sums = sums_h[:, :].rearrange("p (c e) -> p c e", c=KC)
            act.activation(sigw[:, :, 0:EXPERTS], sums, ACT.Sign).then_inc(sig_tiles, 1)
            act.wait_ge(csum_ready, 1)
            act.activation(sigw[:, :, EXPERTS:], csum[:, :, :], ACT.Sign).then_inc(sig_clusters, 1)

            def copy_xt(tile):
                if not tile.exists:
                    return
                g, par = tile.n, tile.par
                wait(act, tok_t, g + 1)
                wait(act, score_done, g - 1)
                act.activation(xt[:, par].rearrange("p c n -> p (c n)"), st_ps[:, par, :], ACT.Copy)\
                    .then_inc(xt_ready, 1)

            def body_rows(i):
                for par in range(2):
                    copy_xt(Tile(i, par, GROUPS, 2))

            passes(act, body_rows, GROUPS // 2)

            def split_high(tile):
                if not tile.exists:
                    return
                t, par = tile.n, tile.par
                wait(act, slot_t, t + 1)
                wait(act, up_done, t - 1)
                for c in range(KC):
                    ins = act.activation(xhl[:, par, 0, c], st_ps[:, par, c * P:(c + 1) * P], ACT.Copy,
                                         scale=wn[:, c:c + 1])
                ins.then_inc(xhi_ready, 1)

            def residual(tile):
                t, par = tile.n, tile.par
                wait(act, gathered[tile.slot], 16 * tile.slot_turn + 16)
                wait(act, res_ready, t - 1)
                act.activation(base[:, par], rows[:, tile.slot, 0:L], ACT.Identity,
                               bias=rows[:, tile.slot, L + 1:L + 2], scale=rows[:, tile.slot, L:L + 1])\
                    .then_inc(base_ready, 1)

            def body_slots(i):
                for k in range(4):
                    split_high(Tile(i, k + 1))
                    residual(Tile(i, k))

            split_high(Tile(0, 0))
            passes(act, body_slots, TILES // 4)

        @block.vector
        def _(dve):
            n = [0]

            def step(ins):
                n[0] += 1
                ins.then_inc(ffn_step, 1)
                dve.wait_ge(ffn_step, n[0])

            sigs = sigw[:, :, :]
            dve.tensor_reduce(mags[:, 0:1], wn[:, :], AX.X, ALU.max, apply_absolute_value=True)\
                .then_inc(mags_ready, 1)
            step(dve.memset(mags[:, 1:2], 0.0))
            dve.tensor_reduce(mags[0:EXPERTS, 1:2], us[0:EXPERTS], AX.X, ALU.max,
                              apply_absolute_value=True)\
                .then_inc(mags_ready, 1)
            dve.wait_ge(sig_tiles, 1)
            dve.tensor_reduce(csum[:, :, :], sigs[:, :, 0:EXPERTS].rearrange(
                "p c (a b) -> p c a b", b=EXPERTS // CLUSTERS), AX.X, ALU.add).then_inc(csum_ready, 1)
            dve.wait_ge(mags_all, 1)
            step(dve.tensor_scalar(powers[:, 0:2], mags[:, 2:4], 2.0 ** -60, None, ALU.max))
            step(dve.tensor_scalar(powers[:, 2:4].bitcast(I32), powers[:, 0:2].bitcast(I32), EXPO, None,
                                   ALU.bitwise_and))
            step(dve.tensor_scalar(powers[:, 4:6].bitcast(I32), powers[:, 2:4].bitcast(I32), -1.0,
                                   float(0x7F000000), ALU.mult, ALU.add))
            step(dve.tensor_scalar(wn[:, :], wn[:, :], powers[:, 4:5], X_SCALE, ALU.mult, ALU.mult))
            step(dve.tensor_scalar(us[0:EXPERTS], us[0:EXPERTS], powers[0:EXPERTS, 5:6], H_SCALE / X_SCALE,
                                   ALU.mult, ALU.mult))
            dve.wait_ge(sig_clusters, 1)
            dve.tensor_tensor(sigs, sigs, wn[:, :].unsqueeze(2).to_broadcast(
                [P, KC, EXPERTS + CLUSTERS]), ALU.mult).then_inc(sig_ready, 1)
            step(dve.tensor_scalar(powers[:, 0:1], powers[:, 2:3], powers[:, 3:4], 1.0 / H_SCALE,
                                   ALU.mult, ALU.mult))
            dve.wait_ge(scale_in, 32)
            dve.tensor_scalar(scale_sb[0:EXPERTS], ds_sb[0:EXPERTS], os_sb[0:EXPERTS, 0:1],
                              powers[0:EXPERTS, 0:1], ALU.mult, ALU.mult).then_inc(sctab_ready, 1)
            dve.wait_ge(cst_in, 16)
            dve.tensor_copy(tri16, cst[:, C_TRI:C_TRI + P])
            dve.memset(ones16, 1.0)

            def copy_scores(tile):
                g, par = tile.n, tile.par
                wait(dve, score_done, g + 1)
                dve.tensor_copy(score[:, bass.ds(g, 1), :].rearrange("p a e -> p (a e)"),
                                banks[par][:, 0:EXPERTS + CLUSTERS]).then_inc(score_copied, 1)

            def body_scores(i):
                for par in range(2):
                    copy_scores(Tile(i, par, GROUPS, 2))

            passes(dve, body_scores, GROUPS // 2)

            def per_tile(col, width):
                return col.unsqueeze(2).to_broadcast([P, GROUPS, width])

            def per_expert(c0, width):
                return cst[:, c0:c0 + width].unsqueeze(1).to_broadcast([P, GROUPS, width])

            top, first, ttop, expert_no, lo_f, hi_f = pick
            tiles_s, clusters_s = score[:, :, 0:EXPERTS], score[:, :, EXPERTS:]
            dve.wait_ge(score_copied, GROUPS)
            step(dve.tensor_reduce(top, clusters_s, AX.X, ALU.max))
            step(dve.tensor_tensor(ckey, clusters_s, per_tile(top, CLUSTERS), ALU.is_lt))
            step(dve.scalar_tensor_tensor(ckey, ckey, 64.0, per_expert(C_CL8, CLUSTERS),
                                          ALU.mult, ALU.add))
            step(dve.tensor_reduce(first, ckey, AX.X, ALU.min))
            a, b = work
            step(dve.tensor_tensor(a, per_expert(C_CL64, EXPERTS), per_tile(first, EXPERTS),
                                   ALU.not_equal))
            step(dve.scalar_tensor_tensor(b, a, -3e38, tiles_s, ALU.mult, ALU.add))
            step(dve.tensor_reduce(ttop, b, AX.X, ALU.max))
            step(dve.tensor_tensor(a, b, per_tile(ttop, EXPERTS), ALU.is_lt))
            step(dve.scalar_tensor_tensor(b, a, 128.0, per_expert(C_E64, EXPERTS),
                                          ALU.mult, ALU.add))
            step(dve.tensor_reduce(expert_no, b, AX.X, ALU.min))
            dve.tensor_tensor(onehot, per_expert(C_E64, EXPERTS), per_tile(expert_no, EXPERTS),
                              ALU.is_equal).then_inc(onehot_ready, 1)

            dve.wait_ge(count_done, 1)
            step(dve.tensor_scalar(counts_i[0:EXPERTS], banks[2][0:EXPERTS, 0:P], float(BLK - 1), None,
                                   ALU.add))
            step(dve.tensor_scalar(counts_i[0:EXPERTS], counts_i[0:EXPERTS], int(math.log2(BLK)), None,
                                   ALU.arith_shift_right))
            dve.tensor_copy(nblk[0:EXPERTS], counts_i[0:EXPERTS]).then_inc(nblk_ready, 1)
            dve.wait_ge(start_done, 1)
            step(dve.tensor_scalar(before[:, 0, :], banks[0][:, 0:EXPERTS], float(BLK), None, ALU.mult))
            dve.wait_ge(nblk_ready, 1)
            step(dve.tensor_tensor(ends[0:EXPERTS], banks[1][0:EXPERTS, 0:P], nblk[0:EXPERTS], ALU.add))
            block_no = cst[0:EXPERTS, C_ROWP:C_ROWP + P]
            step(dve.tensor_tensor(ended[0:EXPERTS], ends[0:EXPERTS], block_no, ALU.is_le))
            dve.tensor_tensor(live[0:EXPERTS], banks[1][0:EXPERTS, 0:P], block_no, ALU.is_le)\
                .then_inc(ended_ready, 1)
            dve.wait_ge(ended_ready, 1)
            dve.tensor_tensor(live[0:EXPERTS], live[0:EXPERTS], ended[0:EXPERTS], ALU.subtract)\
                .then_inc(live_ready, 1)
            dve.wait_ge(rank_done, 1)
            for g in range(1, GROUPS):
                k = g - 1
                step(dve.tensor_tensor(before[:, g, :], before[:, k, :],
                                       st_ps[:, 2 + k // 8, (k % 8) * EXPERTS:(k % 8 + 1) * EXPERTS],
                                       ALU.add))
            dve.wait_ge(expert_done, 1)
            dve.tensor_scalar(expert_of, banks[3][:, 0:BLOCKS], float(EXPERTS - 1), None, ALU.min)\
                .then_inc(expert_ready, 1)
            dve.wait_ge(us_done, 1)
            step(dve.tensor_copy(us_of, banks[1][:, 0:BLOCKS]))
            ranks = st_ps[:, 0:2, :].rearrange("p c (g e) -> p (c g) e", e=EXPERTS)
            step(dve.tensor_tensor(a, before, ranks, ALU.add))
            step(dve.tensor_tensor(b, a, onehot, ALU.mult))
            step(dve.tensor_reduce(top, b, AX.X, ALU.add))
            step(dve.tensor_copy(slot_i[:, 0], top))
            step(dve.tensor_scalar(slot_i[:, 1], slot_i[:, 0], P - 1, None, ALU.bitwise_and))
            step(dve.tensor_scalar(slot_i[:, 2], slot_i[:, 0], int(math.log2(P)), None,
                                   ALU.arith_shift_right))
            step(dve.tensor_copy(lo_f, slot_i[:, 1]))
            step(dve.tensor_copy(hi_f, slot_i[:, 2]))
            step(dve.tensor_tensor(slot_p, per_expert(C_ROWP, P), per_tile(lo_f, P), ALU.is_equal))
            step(dve.tensor_tensor(slot_a, per_expert(C_A32, TILES), per_tile(hi_f, TILES),
                                   ALU.is_equal))
            dve.tensor_tensor(slot_a, slot_a, per_tile(cst[:, C_TOK:C_TOK + GROUPS], TILES), ALU.mult)\
                .then_inc(slots_ready, 1)
            dve.wait_ge(list_done, 1)
            step(dve.tensor_scalar(absent, banks[2][:, 0:TILES], 0.5, 1e6, ALU.is_lt, ALU.mult))
            dve.scalar_tensor_tensor(token_of, banks[2][:, 0:TILES], -1.0, absent, ALU.add, ALU.add)\
                .then_inc(list_ready, 1)

            def split_low(tile):
                if not tile.exists:
                    return
                t, par = tile.n, tile.par
                wait(dve, xhi_ready, t + 1)
                for c in range(KC):
                    ins = dve.scalar_tensor_tensor(xhl[:, par, 1, c], st_ps[:, par, c * P:(c + 1) * P],
                                                   wn[:, c:c + 1], xhl[:, par, 0, c], ALU.mult,
                                                   ALU.subtract)
                ins.then_inc(xlo_ready, 1)

            def hidden(tile):
                t, par = tile.n, tile.par
                wait(dve, up_done, t + 1)
                wait(dve, hlo_ready, t - 1)
                src = hid[:, par].rearrange("p (b n) -> p b n", n=BLK)
                dve.tensor_tensor(src, st_ps[:, 2 + par, 0:P].rearrange("p (b n) -> p b n", n=BLK),
                                  us_of[:, bass.ds(TB * t, TB)].unsqueeze(2).to_broadcast([P, TB, BLK]),
                                  ALU.mult).then_inc(hid_ready, 1)
                high, low = [hz[:, par, k].rearrange("p (b n) -> p b n", n=P + BLK)[:, :, 0:BLK]
                             for k in range(2)]
                wait(dve, hid_ready, t + 1)
                wait(dve, down_done, t - 1)
                settle(dve)
                dve.tensor_scalar(high, src, 0.0, None, ALU.max).then_inc(hhi_ready, 1)
                wait(dve, hhi_ready, t + 1)
                dve.scalar_tensor_tensor(low, src, 0.0, high, ALU.max, ALU.subtract)\
                    .then_inc(hlo_ready, 1)

            def scaled(tile):
                if not tile.exists:
                    return
                t, par = tile.n, tile.par
                wait(dve, down_done, t + 1)
                wait(dve, scl_in[par], 16 * TB * (tile.turn + 1))
                wait(dve, scattered[tile.slot], 16 * tile.slot_turn)
                dve.tensor_tensor(res[:, tile.slot], banks[par], scl[:, par], ALU.mult)\
                    .then_inc(prod_ready, 1)
                wait(dve, prod_ready, t + 1)
                wait(dve, base_ready, t + 1)
                dve.tensor_tensor(res[:, tile.slot], res[:, tile.slot], base[:, par], ALU.add)\
                    .then_inc(res_ready, 1)

            def body_slots(i):
                for k in range(4):
                    split_low(Tile(i, k + 1))
                    hidden(Tile(i, k))
                    scaled(Tile(i, k - 1))

            dve.wait_ge(clean, 3)
            dve.wait_ge(expert_ready, 1)
            split_low(Tile(0, 0))
            passes(dve, body_slots, TILES // 4, first=2)
            scaled(Tile(TILES // 4 - 1, 3))

        @block.gpsimd
        def _(pool):
            pool.wait_ge(mags_ready, 2)
            pool.partition_all_reduce(mags[:, 2:4], mags[:, 0:2], P, ABSMAX).then_inc(mags_all, 1)
            pool.memset(rows[:, 2:4], 0.0).then_inc(clean, 1)
            pool.memset(hz[:, 0], 0.0).then_inc(clean, 1)
            pool.memset(hz[:, 1], 0.0).then_inc(clean, 1)
            pool.wait_ge(clean, 3)
            pool.wait_ge(tok_t, GROUPS)

            def gather(tile):
                if not tile.exists:
                    return
                t, k = tile.n, tile.slot
                wait(pool, slot_t, t - 3)
                wait(pool, base_ready, t - 3)
                settle(pool)
                pool.tensor_copy(gidx[:, k:k + 1], token_of[:, bass.ds(t, 1)]).then_inc(gidx_ready, 1)
                wait(pool, gidx_ready, t + 1)
                settle(pool)
                pool.indirect_dma_start(
                    rows[:, k], None, ytab.rearrange("g p n -> (g p) n"),
                    bass.IndirectOffsetOnAxis(ap=gidx[:, k:k + 1], axis=0),
                    bounds_check=TOKENS - 1, oob_is_err=False).then_inc(gathered[k], 16)

            def finish(tile):
                if not tile.exists:
                    return
                t, k = tile.n, tile.slot
                wait(pool, scattered[k], 16 * tile.slot_turn)
                settle(pool)
                pool.tensor_copy(sidx[:, k:k + 1], token_of[:, bass.ds(t, 1)]).then_inc(sidx_ready, 1)
                wait(pool, sidx_ready, t + 1)
                wait(pool, res_ready, t + 1)
                settle(pool)
                pool.indirect_dma_start(
                    out, bass.IndirectOffsetOnAxis(ap=sidx[:, k:k + 1], axis=0),
                    res[:, k], None, bounds_check=TOKENS - 1, oob_is_err=False)\
                    .then_inc(scattered[k], 16)

            def body_slots(i):
                for k in range(4):
                    gather(Tile(i, k + 3))
                    finish(Tile(i, k - 1))

            pool.wait_ge(list_ready, 1)
            for k in range(3):
                gather(Tile(0, k))
            passes(pool, body_slots, TILES // 4, first=2, last=1)
            finish(Tile(TILES // 4 - 1, 3))
            for k in range(4):
                pool.wait_ge(scattered[k], 16 * (TILES // 4))


_INS = ["x", "ctx_k", "ctx_v", "klen", "up_h", "dn_h", "us_h", "ds_h", "os_h", "w_h", "cst_h"]


def lay_out(i):
    import numpy as np

    a = {k: np.asarray(v) for k, v in i.items()}
    ctx = a["ctx_2048"]
    up, dn = a["L0_ffn_up_w"], a["L0_ffn_down_w"]
    return {
        "x": a["x"].reshape(GROUPS, P, L),
        "ctx_k": ctx.reshape(GROUPS, P, L),
        "ctx_v": ctx.reshape(GROUPS, 2, 2, HD, KC, P).transpose(0, 2, 5, 4, 1, 3).reshape(
            GROUPS, 2, P, KC * 2, HD),
        "klen": a["itok_B_779_1933"],
        "up_h": up.reshape(8, 8, HID, KC, P).transpose(3, 0, 4, 1, 2).reshape(NUP, P, CH),
        "dn_h": dn.reshape(NUP, 2, L, HID).transpose(0, 3, 1, 2).reshape(NUP, P, CH),
        "us_h": a["L0_ffn_up_scale"],
        "ds_h": a["L0_ffn_down_scale"],
        "os_h": a["L0_ffn_output_scale"].reshape(EXPERTS, 1),
        "w_h": a["L0_ffn_norm_weight"].reshape(KC, P).T,
        "cst_h": constants(),
    }


def kernel(**inputs):
    import numpy as np
    import concourse.bacc as bacc
    from concourse.bass_utils import run_bass_kernel_spmd

    nc = bacc.Bacc("TRN2", target_bir_lowering=False, num_devices=1)
    arrays, args = {}, []
    laid = lay_out(inputs)
    for name in _INS:
        arr = np.ascontiguousarray(laid[name])
        arrays[f"in_{name}"] = arr
        args.append(nc.dram_tensor(f"in_{name}", arr.shape, mybir.dt.from_np(arr.dtype),
                                   kind="ExternalInput").ap())
    out = nc.dram_tensor("out_0", (TOKENS, L), F32, kind="ExternalOutput").ap()
    split_d = nc.dram_tensor("split_d", (GROUPS, P, 4, L), F16, kind="Internal").ap()
    ytab = nc.dram_tensor("ytab", (GROUPS, P, YROW), F32, kind="Internal").ap()
    sctab = nc.dram_tensor("sctab", (EXPERTS, L), F32, kind="Internal").ap()
    build(nc, *args, out, split_d, ytab, sctab)
    res = run_bass_kernel_spmd(nc, [arrays], core_ids=[0])
    return res.results[0]["out_0"].reshape(B, C, L)
```

```python
import math
from contextlib import ExitStack

import concourse.bass as bass
from concourse import mybir

F32 = mybir.dt.float32
F16 = mybir.dt.float16
BF16 = mybir.dt.bfloat16
I32 = mybir.dt.int32
U32 = mybir.dt.uint32
ALU = mybir.AluOpType
ACT = mybir.ActivationFunctionType
AX = mybir.AxisListType
ABSMAX = bass.bass_isa.ReduceOp.absmax

P = 128
B, C, L = 8, 256, 512
HD = 32
HEADS = B * C // HD
GROUPS = B * C // P
GH = P // HD
KC = L // P
EXPERTS, HID = 64, 128
CLUSTERS = 8
BLK = 32
BLOCKS = 128
TOKENS = GROUPS * P
TILES = BLOCKS * BLK // P
TB = P // BLK
CH = 1024
NUP = EXPERTS * HID * KC // CH
ATT_SCALE = 1.0 / (64 ** 0.5 * math.log(20))
LN_EPS, RMS_EPS = 1e-5, 1e-6
ARENA = 19800
EXPO = 0x7F800000
Q_SCALE = 8.0
K_SCALE = 4096.0
X_SCALE = 512.0
H_SCALE = 16.0
LN1_STEPS, LN2_STEPS = 5, 13
YROW = L + 4

C_ID, C_TRI, C_ROWP, C_SELP = 0, 128, 256, 384
C_E64, C_CL64, C_ONES, C_A32, C_SELA, C_TOK, C_P, C_CL8, C_END = 512, 576, 640, 768, 800, 832, 848, 849, 857


def constants():
    import numpy as np

    c = np.zeros((P, C_END), np.float32)
    p, r = np.arange(P)[:, None], np.arange(P)[None, :]
    c[:, C_ID:C_ID + P] = p == r
    c[:, C_TRI:C_TRI + P] = p < r
    c[:, C_ROWP:C_ROWP + P] = r
    c[:, C_SELP:C_SELP + P] = p % TB == r // BLK
    c[:, C_E64:C_E64 + EXPERTS] = np.arange(EXPERTS)
    c[:, C_CL64:C_CL64 + EXPERTS] = np.arange(EXPERTS) // CLUSTERS
    c[:, C_ONES:C_ONES + P] = 1
    c[:, C_A32:C_A32 + TILES] = np.arange(TILES)
    c[:, C_SELA:C_SELA + TILES] = p // TB == np.arange(TILES)[None, :]
    c[:, C_TOK:C_TOK + GROUPS] = p + P * np.arange(GROUPS)[None, :] + 1
    c[:, C_P:C_P + 1] = p
    c[:, C_CL8:C_CL8 + CLUSTERS] = np.arange(CLUSTERS)
    return c


def build(nc, x, ctx_k, ctx_v, klen, up_h, dn_h, us_h, ds_h, os_h, w_h, cst_h, out,
          split_d, inv_d, ytab, sctab):
    stack = ExitStack()
    with stack:
        def sb(name, shape, dt):
            return stack.enter_context(nc.sbuf_tensor(name, shape, dt))

        def sem(name):
            return stack.enter_context(nc.semaphore(name))

        w_up = sb("w_up", [P, KC, EXPERTS, HID], BF16)
        w_dn = sb("w_dn", [P, EXPERTS, L], BF16)
        ident16 = sb("ident16", [P, P], F16)
        sums_h = sb("sums_h", [P, KC * EXPERTS], F32)
        expscale = sb("expscale", [P, GROUPS], F32)
        small = sb("small", [P, 4], F32)
        us = sb("us", [P, HID], F32)
        wn = sb("wn", [P, KC], F32)

        arena = sb("arena", [P, ARENA], F32)
        used = [0, 0]

        def carve(phase, words):
            a = used[phase]
            used[phase] += words
            assert used[phase] <= ARENA, used
            return arena[:, a:a + words]

        stage = carve(0, 2 * CH).rearrange("p (s n) -> p s n", s=2)
        pt = carve(0, 2 * KC * L).rearrange("p (s c q) -> p s c q", s=2, c=KC)
        qst = carve(0, 2 * GH * L // 2).bitcast(F16).rearrange("p (g j q) -> p g j q", g=2, j=GH)
        kst = carve(0, 2 * GH * L // 2).bitcast(F16).rearrange("p (g j q) -> p g j q", g=2, j=GH)
        vt = carve(0, 2 * KC * 2 * 7 * HD).rearrange("p (g c k n) -> p g c k n", g=2, c=KC, k=2)
        xin = carve(0, L)
        kin = carve(0, L)
        parts = carve(0, 4 * L // 2).bitcast(F16).rearrange("p (s q) -> p s q", s=4)
        xres = carve(0, 2 * L).rearrange("p (s q) -> p s q", s=2)
        att = carve(0, 2 * L).rearrange("p (s q) -> p s q", s=2)
        rden = carve(0, 2 * L).rearrange("p (s q) -> p s q", s=2)
        ident_in = rden[:, 0, 0:P]
        ytile = carve(0, YROW)
        dcol = carve(0, GH * L // P)
        mx = sb("mx", [P, 2, KC], F32)
        mhl = sb("mhl", [P, 2, KC, 2], F16)
        stat = sb("stat", [P, 6], F32)
        mv = sb("mv", [P, 2], F32)
        stat2 = sb("stat2", [P, 6], F32)
        mv2 = sb("mv2", [P, 2], F32)
        sml = sb("sml", [P, 16], F32)
        sm2 = sb("sm2", [P, 16], F32)
        kpow = sb("kpow", [P, 4], F32)
        halves = sb("halves", [P, 2], F32)
        lnk = sb("lnk", [P, B], F32)
        klen_i = sb("klen_i", [P, B], I32)

        cst = carve(1, C_END)
        ident = cst[:, C_ID:C_ID + P]
        rows = carve(1, 4 * YROW).rearrange("p (s n) -> p s n", s=4)
        sigw = carve(1, KC * (EXPERTS + CLUSTERS)).rearrange("p (c e) -> p c e", c=KC)
        csum = carve(1, KC * CLUSTERS).rearrange("p (c e) -> p c e", c=KC)
        ds_sb = carve(1, L)
        os_sb = carve(1, 1)
        scale_sb = carve(1, L)
        mags = carve(1, 4)
        powers = carve(1, 6)
        xt = carve(1, 2 * L).rearrange("p (s c n) -> p s c n", s=2, c=KC)
        score = carve(1, 4 * (EXPERTS + CLUSTERS)).rearrange("p (g e) -> p g e", g=4)
        near = carve(1, 8 * EXPERTS).rearrange("p (k g e) -> p k g e", k=2, g=4)
        ckey = carve(1, 4 * CLUSTERS).rearrange("p (g e) -> p g e", g=4)
        before = carve(1, GROUPS * EXPERTS).rearrange("p (g e) -> p g e", g=GROUPS)
        onehot = carve(1, GROUPS * EXPERTS // 2).bitcast(F16).rearrange("p (g e) -> p g e", g=GROUPS)
        pick = [carve(1, 4) for _ in range(4)]
        slot_f, lo_f, hi_f = [carve(1, GROUPS) for _ in range(3)]
        counts = carve(1, P)
        counts_i = carve(1, P).bitcast(I32)
        nblk = carve(1, P // 2).bitcast(F16)
        ends = carve(1, P)
        ended = carve(1, P // 2).bitcast(F16)
        slot_i = carve(1, 3 * GROUPS).bitcast(I32).rearrange("p (k g) -> p k g", k=3)
        slot_p = carve(1, GROUPS * P // 2).bitcast(F16).rearrange("p (g n) -> p g n", g=GROUPS)
        slot_a = carve(1, GROUPS * TILES // 2).bitcast(F16).rearrange("p (g n) -> p g n", g=GROUPS)
        tri16 = carve(1, P // 2).bitcast(F16)
        ones16 = carve(1, P // 2).bitcast(F16)
        absent = carve(1, TILES)
        token_of = carve(1, TILES).bitcast(I32)
        expert_of = carve(1, BLOCKS).bitcast(I32)
        gidx = carve(1, 4).bitcast(I32)
        sidx = carve(1, 4).bitcast(I32)
        xhl = carve(1, 2 * L).bitcast(F16).rearrange("p (s h c n) -> p s h c n", s=2, h=2, c=KC)
        hparts = carve(1, 4 * P).rearrange("p (s b n) -> p s b n", s=2, b=TB)
        hid = carve(1, 2 * P).rearrange("p (s n) -> p s n", s=2)
        DIAG = TB * (P + BLK)
        hz = carve(1, 2 * DIAG).bitcast(F16).rearrange("p (s h n) -> p s h n", s=2, h=2)
        scl = carve(1, 2 * L).rearrange("p (s n) -> p s n", s=2)
        base = carve(1, 2 * L).rearrange("p (s n) -> p s n", s=2)
        res = carve(1, 4 * L).rearrange("p (s n) -> p s n", s=4)
        work = [res.rearrange("p s n -> p (s n)")[:, k * GROUPS * EXPERTS:(k + 1) * GROUPS * EXPERTS]
                .rearrange("p (g e) -> p g e", g=GROUPS) for k in range(2)]
        live = carve(1, P)
        us_of = carve(1, BLOCKS)

        sq_ps = stack.enter_context(nc.psum_tensor("sq_ps", [P, 2, L], F32))
        pv_ps = stack.enter_context(nc.psum_tensor("pv_ps", [P, L], F32))
        mt_ps = stack.enter_context(nc.psum_tensor("mt_ps", [P, L], F32))
        st_ps = stack.enter_context(nc.psum_tensor("st_ps", [P, 4, L], F32))
        banks = [sq_ps[:, 0, :], sq_ps[:, 1, :], pv_ps[:, :], mt_ps[:, :]]

        const_in = sem("const_in")
        setup_dve = sem("setup_dve")
        setup_pool = sem("setup_pool")
        lnk_ready = sem("lnk_ready")
        consts_ready = sem("consts_ready")
        sctab_out = sem("sctab_out")
        xk_in = sem("xk_in")
        v_in = sem("v_in")
        xres_in = sem("xres_in")
        stats_ready = sem("stats_ready")
        moments_ready = sem("moments_ready")
        kmax_ready = sem("kmax_ready")
        kmax_all = sem("kmax_all")
        ln1_step = sem("ln1_step")
        kpow_step = sem("kpow_step")
        q_ready = sem("q_ready")
        hi_ready = sem("hi_ready")
        parts_ready = sem("parts_ready")
        split_out = sem("split_out")
        stack_in = sem("stack_in")
        sq_done = sem("sq_done")
        max_done = sem("max_done")
        mhi_done = sem("mhi_done")
        mneg_done = sem("mneg_done")
        mrow_done = sem("mrow_done")
        mrow_copied = sem("mrow_copied")
        st_done = sem("st_done")
        exp_done = sem("exp_done")
        pv_done = sem("pv_done")
        dcol_in = sem("dcol_in")
        inverted = sem("inverted")
        inv_out = sem("inv_out")
        rden_in = sem("rden_in")
        att_evac = sem("att_evac")
        ratio_done = sem("ratio_done")
        x2_done = sem("x2_done")
        stats2_ready = sem("stats2_ready")
        moments2_ready = sem("moments2_ready")
        ln2_step = sem("ln2_step")
        y_done = sem("y_done")
        y_out = sem("y_out")
        w_in = [sem("w_in0"), sem("w_in1")]
        sign_done = sem("sign_done")
        sums_done = sem("sums_done")

        scale_in = sem("scale_in")
        mags_ready = sem("mags_ready")
        mags_all = sem("mags_all")
        ffn_step = sem("ffn_step")
        sig_tiles = sem("sig_tiles")
        csum_ready = sem("csum_ready")
        sig_clusters = sem("sig_clusters")
        sig_ready = sem("sig_ready")
        sctab_ready = sem("sctab_ready")
        row_in = [sem(f"row_in{k}") for k in range(4)]
        tok_t = sem("tok_t")
        xt_ready = sem("xt_ready")
        score_done = sem("score_done")
        score_copied = sem("score_copied")
        onehot_ready = sem("onehot_ready")
        rank_done = sem("rank_done")
        count_done = sem("count_done")
        nblk_ready = sem("nblk_ready")
        start_done = sem("start_done")
        ended_ready = sem("ended_ready")
        expert_done = sem("expert_done")
        expert_ready = sem("expert_ready")
        slots_ready = sem("slots_ready")
        list_done = sem("list_done")
        list_ready = sem("list_ready")
        clean = sem("clean")
        gidx_ready = sem("gidx_ready")
        sidx_ready = sem("sidx_ready")
        gathered = [sem(f"gathered{k}") for k in range(4)]
        slot_t = sem("slot_t")
        xhi_ready = sem("xhi_ready")
        xlo_ready = sem("xlo_ready")
        up_done = sem("up_done")
        live_ready = sem("live_ready")
        us_done = sem("us_done")
        hid_ready = sem("hid_ready")
        hhi_ready = sem("hhi_ready")
        hlo_ready = sem("hlo_ready")
        down_done = sem("down_done")
        scl_in = [sem("scl_in0"), sem("scl_in1")]
        base_ready = sem("base_ready")
        prod_ready = sem("prod_ready")
        res_ready = sem("res_ready")
        scattered = [sem(f"scattered{k}") for k in range(4)]
        cst_in = sem("cst_in")
        routed = sem("routed")
        hsum_ready = sem("hsum_ready")

        def wait(eng, s, v):
            if not (isinstance(v, int) and v <= 0):
                eng.wait_ge(s, v)

        class Head:

            def __init__(self, i, jj):
                self.n, self.j, self.slot = 8 * i + jj, jj % GH, jj % 2
                self.g, self.par = 2 * i + jj // GH, jj // GH % 2
                self.pair = 4 * i + jj // 2
                self.exists = not isinstance(i, int) or 0 <= self.n < HEADS

        def settle(eng):
            eng.sem_inc(settled[eng.engine], 1)

        def ok(g):
            return not isinstance(g, int) or 0 <= g < GROUPS

        def bodies(eng, body, first=1, last=1):
            for i in range(first):
                body(i)
            with eng.Fori(first, B - last) as i:
                body(i)
            for i in range(B - last, B):
                body(i)

        settled = {e.engine: sem(f"settled{k}") for k, e in enumerate(
            (nc.scalar, nc.vector, nc.gpsimd, nc.sync, nc.tensor))}
        attention = ExitStack()
        block = attention.enter_context(nc.Block())

        @block.sync
        def _(sp):
            sp.dma_start(ident_in, cst_h[:, C_ID:C_ID + P]).then_inc(const_in, 16)
            sp.dma_start(klen_i[:, :], bass.AP(klen.tensor, 0, [[0, P], [1, B]])).then_inc(const_in, 16)
            sp.dma_start(us[0:EXPERTS, :], us_h).then_inc(const_in, 16)
            sp.dma_start(wn[:, :], w_h).then_inc(const_in, 16)

            def load_in(g):
                if not ok(g):
                    return
                wait(sp, parts_ready, 2 * g)
                sp.dma_start(xin, x[bass.ds(g, 1)].rearrange("a p q -> (a p) q")).then_inc(xk_in, 16)
                sp.dma_start(kin, ctx_k[bass.ds(g, 1)].rearrange("a p q -> (a p) q")).then_inc(xk_in, 16)

            def put_parts(g):
                if not ok(g):
                    return
                wait(sp, parts_ready, 2 * (g + 1))
                sp.dma_start(split_d[bass.ds(g, 1)].rearrange("a p s q -> (a p) s q"), parts)\
                    .then_inc(split_out, 16)

            def load_stacks(g, par):
                if not ok(g):
                    return
                counts = [16 * (g + 1), 8 * (g - 1)]
                if not isinstance(g, int):
                    counts = [sp.snap(c) for c in counts]
                wait(sp, split_out, counts[0])
                settle(sp)
                wait(sp, st_done, counts[1])
                src = split_d[bass.ds(g, 1)].rearrange("a (j d) s q -> d (a j) s q", j=GH)
                for r, (sq, sk) in enumerate(((0, 2), (0, 3), (1, 2))):
                    rows = slice(r * HD, (r + 1) * HD)
                    sp.dma_start(qst[rows, par], src[:, :, sq]).then_inc(stack_in, 16)
                    sp.dma_start(kst[rows, par], src[:, :, sk]).then_inc(stack_in, 16)

            def load_v(g, par):
                if not ok(g):
                    return
                wait(sp, pv_done, 4 * (g - 1))
                for e in range(2):
                    sp.dma_start(
                        vt[:, par, :, :, e * 4 * HD:(e * 4 + 1) * HD].rearrange("p c k n -> p (c k) n"),
                        ctx_v[bass.ds(g, 1), e].rearrange("a p c n -> (a p) c n")).then_inc(v_in, 16)

            def load_res(g, par):
                wait(sp, x2_done, g - 1)
                sp.dma_start(xres[:, par], x[bass.ds(g, 1)].rearrange("a p q -> (a p) q"))\
                    .then_inc(xres_in, 16)

            def collect_den(g, par):
                if not ok(g):
                    return
                wait(sp, att_evac, 2 * g + 2)
                sp.dma_start(dcol, rden[0:P:HD, par, :]).then_inc(dcol_in, 16)

            def spread_inverses(g, par):
                if not ok(g):
                    return
                wait(sp, inverted, g + 1)
                sp.dma_start(inv_d.rearrange("j (k c) -> (j k) c", c=GH * L // P), dcol)\
                    .then_inc(inv_out, 16)
                wait(sp, inv_out, 16 * g + 16)
                sp.dma_start(rden[:, par, :], bass.AP(inv_d.tensor, 0, [[L, GH], [0, HD], [1, L]]))\
                    .then_inc(rden_in, 16)

            def put_y(g):
                if not ok(g):
                    return
                wait(sp, y_done, g + 1)
                sp.dma_start(ytab[bass.ds(g, 1)].rearrange("a p q -> (a p) q"), ytile)\
                    .then_inc(y_out, 16)

            load_in(0)
            put_parts(0)
            load_in(1)
            load_stacks(0, 0)
            sp.wait_ge(setup_pool, 1)
            load_v(0, 0)
            put_parts(1)
            load_in(2)
            load_stacks(1, 1)

            def body(i):
                for par in range(2):
                    g = 2 * i + par
                    load_res(g, par)
                    load_v(g + 1, 1 - par)
                    collect_den(g - 1, 1 - par)
                    spread_inverses(g - 1, 1 - par)
                    put_parts(g + 2)
                    load_in(g + 3)
                    put_y(g - 2)
                    load_stacks(g + 2, par)

            bodies(sp, body, last=2)
            collect_den(GROUPS - 1, 1)
            spread_inverses(GROUPS - 1, 1)
            put_y(GROUPS - 2)
            put_y(GROUPS - 1)

        @block.tensor
        def _(pe):
            def scores_q(h, half):
                if not h.exists:
                    return
                if h.j == 0 and half == 0:
                    wait(pe, stack_in, 96 * h.g + 96)
                wait(pe, max_done, 2 * h.n + half)
                for t in range(2):
                    q = (2 * half + t) * P
                    mm = pe.matmul(sq_ps[:, t, :], qst[0:96, h.par, h.j, q:q + P],
                                   kst[0:96, h.par, h.j, :], start=True, stop=True)
                mm.then_inc(sq_done, 1)

            def max_rows(h):
                if not h.exists:
                    return
                wait(pe, mneg_done, h.n + 1)
                wait(pe, mrow_copied, h.n)
                for t in range(KC):
                    mm = pe.matmul(mt_ps[96:98, t * P:(t + 1) * P], mhl[:, h.slot, t, :], ident16[:, :],
                                   start=True, stop=True)
                mm.then_inc(mrow_done, 1)

            def scores_k(h, half):
                wait(pe, mrow_copied, h.n + 1)
                wait(pe, exp_done, 2 * h.n - 1 + half)
                for c in (2 * half, 2 * half + 1):
                    mm = pe.matmul(st_ps[:, c, :], kst[0:98, h.par, h.j, c * P:(c + 1) * P],
                                   qst[0:98, h.par, h.j, :], start=True, stop=True)
                mm.then_inc(st_done, 1)

            def values(h, half):
                if not h.exists:
                    return
                if half == 0 and h.j == 0:
                    wait(pe, v_in, 32 * h.g + 32)
                if half == 0 and h.slot == 0:
                    wait(pe, att_evac, h.pair)
                wait(pe, exp_done, 2 * h.n + 1 + half)
                e = h.slot
                for c in (2 * half, 2 * half + 1):
                    mm = pe.matmul(pv_ps[:, :], vt[:, h.par, c, h.j // 2, 3 * HD * e:3 * HD * e + P],
                                   pt[:, h.slot, c, :], start=(e == 0 and c == 0),
                                   stop=(e == 1 and c == KC - 1))
                if half == 1:
                    mm.then_inc(pv_done, 1)

            pe.wait_ge(consts_ready, 3)
            for off in (0, 1):
                for half in range(2):
                    scores_q(Head(0, off), half)
            max_rows(Head(0, 0))

            def body(i):
                for jj in range(2 * GH):
                    scores_k(Head(i, jj), 0)
                    scores_q(Head(i, jj + 2), 0)
                    values(Head(i, jj - 1), 0)
                    scores_k(Head(i, jj), 1)
                    max_rows(Head(i, jj + 1))
                    scores_q(Head(i, jj + 2), 1)
                    values(Head(i, jj - 1), 1)

            bodies(pe, body)
            values(Head(B - 1, 7), 0)
            values(Head(B - 1, 7), 1)

        @block.scalar
        def _(act):
            def load_w(h):
                if not h.exists:
                    return
                wait(act, sign_done, h.n - 1)
                act.dma_start(stage[:, h.slot], (up_h, dn_h)[h.slot][bass.ds(h.pair, 1)]
                              .rearrange("a p n -> (a p) n")).then_inc(w_in[h.slot], 16)

            load_w(Head(0, 0))
            load_w(Head(0, 1))
            act.wait_ge(setup_dve, 1)
            act.activation(lnk[:, :], lnk[:, :], ACT.Ln).then_inc(lnk_ready, 1)

            def norm_q(g):
                if not ok(g):
                    return
                wait(act, ln1_step, LN1_STEPS * g + LN1_STEPS)
                act.activation(xin, xin, ACT.Identity, bias=sml[:, 3:4], scale=sml[:, 2:3])\
                    .then_inc(q_ready, 1)

            def copy_rows(h):
                if not h.exists:
                    return
                wait(act, mrow_done, h.n + 1)
                act.activation(qst[96:98, h.par, h.j, :], mt_ps[96:98, :], ACT.Copy)\
                    .then_inc(mrow_copied, 1)

            def exps(h, half):
                wait(act, st_done, 2 * h.n + 1 + half)
                wait(act, pv_done, h.n - 1)
                settle(act)
                act.activation(pt[:, h.slot, 2 * half:2 * half + 2, :], st_ps[:, 2 * half:2 * half + 2, :],
                               ACT.Exp, scale=expscale[:, bass.ds(h.g, 1)]).then_inc(exp_done, 1)

            def evacuate(h):
                if not h.exists:
                    return
                rows = slice(64 * (h.j // 2), 64 * (h.j // 2) + 64)
                wait(act, pv_done, h.n + 1)
                if h.j == 1:
                    wait(act, y_done, h.g - 1)
                act.activation(rden[rows, h.par], pv_ps[64:128, :], ACT.Copy)
                act.activation(att[rows, h.par], pv_ps[0:64, :], ACT.Copy).then_inc(att_evac, 1)

            def signs(h):
                wait(act, w_in[h.slot], 16 * h.pair + 16)
                dst = (w_up[:, :, :, :].rearrange("p c e h -> p (c e h)"),
                       w_dn[:, :, :].rearrange("p e n -> p (e n)"))[h.slot]
                act.activation(dst[:, bass.ds(h.pair * CH, CH)], stage[:, h.slot], ACT.Sign)\
                    .then_inc(sign_done, 1)

            def norm_y(g, par):
                if not ok(g):
                    return
                wait(act, ln2_step, LN2_STEPS * g + LN2_STEPS)
                act.activation(ytile[:, 0:L], att[:, par], ACT.Identity, bias=sm2[:, 7:8],
                               scale=sm2[:, 6:7]).then_inc(y_done, 1)

            norm_q(0)
            norm_q(1)
            copy_rows(Head(0, 0))

            def body(i):
                for jj in range(2 * GH):
                    h = Head(i, jj)
                    exps(h, 0)
                    copy_rows(Head(i, jj + 1))
                    exps(h, 1)
                    signs(h)
                    if h.slot == 0:
                        evacuate(Head(i, jj - 1))
                    if h.j == 1:
                        norm_q(h.g + 2)
                        norm_y(h.g - 2, h.par)
                    load_w(Head(i, jj + 2))

            bodies(act, body)
            evacuate(Head(B - 1, 7))
            norm_y(GROUPS - 2, 0)
            norm_y(GROUPS - 1, 1)

        @block.vector
        def _(dve):
            dve.wait_ge(const_in, 64)
            dve.tensor_copy(lnk[:, :], klen_i[:, :]).then_inc(setup_dve, 1)
            dve.tensor_copy(ident16[:, :], ident_in).then_inc(consts_ready, 1)
            dve.memset(kst[96:98, 0, :, :], K_SCALE).then_inc(consts_ready, 1)
            dve.memset(kst[96:98, 1, :, :], K_SCALE).then_inc(consts_ready, 1)
            dve.wait_ge(lnk_ready, 1)
            dve.tensor_scalar(lnk[:, :], lnk[:, :], ATT_SCALE / (Q_SCALE * K_SCALE), None, ALU.mult)\
                .then_inc(setup_dve, 1)

            def prep_stats(g):
                if not ok(g):
                    return
                wait(dve, xk_in, 32 * g + 32)
                dve.bn_stats(stat[:, :], xin).then_inc(stats_ready, 1)
                wait(dve, kpow_step, 4 * g)
                dve.tensor_reduce(small[:, 0:1], kin, AX.X, ALU.max, apply_absolute_value=True)\
                    .then_inc(kmax_ready, 1)
                wait(dve, stats_ready, g + 1)
                wait(dve, q_ready, g)
                settle(dve)
                dve.bn_aggr(mv[:, :], stat[:, :]).then_inc(moments_ready, 1)

            def prep_kpow(g, b):
                if not ok(g):
                    return
                wait(dve, kmax_all, g + 1)
                dve.tensor_scalar(kpow[:, 0:1], small[:, 1:2], 2.0 ** -60, None, ALU.max)\
                    .then_inc(kpow_step, 1)
                wait(dve, kpow_step, 4 * g + 1)
                dve.tensor_scalar(kpow[:, 1:2].bitcast(I32), kpow[:, 0:1].bitcast(I32), EXPO, None,
                                  ALU.bitwise_and).then_inc(kpow_step, 1)
                wait(dve, kpow_step, 4 * g + 2)
                dve.tensor_scalar(kpow[:, 2:3].bitcast(I32), kpow[:, 1:2].bitcast(I32), -1.0,
                                  float(0x7F000000 + (12 << 23)), ALU.mult, ALU.add)\
                    .then_inc(kpow_step, 1)
                wait(dve, setup_dve, 2)
                dve.tensor_tensor(expscale[:, bass.ds(g, 1)], kpow[:, 1:2], lnk[:, bass.ds(b, 1)],
                                  ALU.mult).then_inc(kpow_step, 1)

            def prep_k(g):
                if not ok(g):
                    return
                wait(dve, kpow_step, 4 * g + 3)
                wait(dve, split_out, 16 * g)
                dve.tensor_scalar(parts[:, 2], kin, kpow[:, 2:3], None, ALU.mult).then_inc(hi_ready, 1)
                wait(dve, hi_ready, 2 * g + 1)
                dve.scalar_tensor_tensor(parts[:, 3], kin, kpow[:, 2:3], parts[:, 2], ALU.mult,
                                         ALU.subtract).then_inc(parts_ready, 1)

            def prep_q(g):
                if not ok(g):
                    return
                wait(dve, q_ready, g + 1)
                dve.tensor_copy(parts[:, 0], xin).then_inc(hi_ready, 1)
                wait(dve, hi_ready, 2 * g + 2)
                dve.tensor_tensor(parts[:, 1], xin, parts[:, 0], ALU.subtract).then_inc(parts_ready, 1)

            def reduce_scores(h, half):
                if not h.exists:
                    return
                if half == 0:
                    wait(dve, mneg_done, h.n - 1)
                wait(dve, sq_done, 2 * h.n + half + 1)
                dve.tensor_reduce(mx[:, h.slot, 2 * half:2 * half + 2], sq_ps[:, :, :], AX.X,
                                  ALU.max, negate=True).then_inc(max_done, 1)

            def split_maxima(h):
                if not h.exists:
                    return
                wait(dve, max_done, 2 * h.n + 2)
                wait(dve, mrow_done, h.n - 1)
                dve.tensor_scalar(mhl[:, h.slot, :, 0], mx[:, h.slot, :], 1.0 / K_SCALE, None, ALU.mult)\
                    .then_inc(mhi_done, 1)
                wait(dve, mhi_done, h.n + 1)
                dve.scalar_tensor_tensor(mhl[:, h.slot, :, 1], mx[:, h.slot, :], 1.0 / K_SCALE,
                                         mhl[:, h.slot, :, 0], ALU.mult, ALU.subtract)\
                    .then_inc(mneg_done, 1)

            def invert(g):
                if not ok(g):
                    return
                wait(dve, dcol_in, 16 * g + 16)
                dve.reciprocal(dcol, dcol).then_inc(inverted, 1)

            def stats2(g, par):
                if not ok(g):
                    return
                wait(dve, x2_done, g + 1)
                dve.bn_stats(stat2[:, :], att[:, par]).then_inc(stats2_ready, 1)
                wait(dve, stats2_ready, g + 1)
                wait(dve, ln2_step, LN2_STEPS * g)
                settle(dve)
                dve.bn_aggr(mv2[:, :], stat2[:, :]).then_inc(moments2_ready, 1)

            def sum_signs(h):
                if not h.exists:
                    return
                k = h.pair
                wait(dve, sign_done, 2 * k + 1)
                src = w_up[:, :, :, :].rearrange("p c e h -> p (c e h)")
                dve.tensor_reduce(sums_h[:, bass.ds(8 * k, 8)],
                                  src[:, bass.ds(k * CH, CH)].rearrange("p (e h) -> p e h", h=HID),
                                  AX.X, ALU.add).then_inc(sums_done, 1)

            for g in range(2):
                prep_stats(g)
                prep_kpow(g, 0)
                prep_k(g)
                prep_q(g)
            for jj in range(2):
                for half in range(2):
                    reduce_scores(Head(0, jj), half)
                split_maxima(Head(0, jj))

            def body(i):
                for jj in range(2 * GH):
                    h = Head(i, jj)
                    reduce_scores(Head(i, jj + 2), 0)
                    if h.j == 0:
                        prep_stats(h.g + 2)
                    if h.j == 1:
                        prep_kpow(h.g + 2, i + 1)
                        prep_k(h.g + 2)
                    if h.j == 2:
                        invert(h.g - 1)
                    reduce_scores(Head(i, jj + 2), 1)
                    split_maxima(Head(i, jj + 2))
                    if h.j == 0:
                        stats2(h.g - 2, h.par)
                    if h.j == 2:
                        prep_q(h.g + 2)
                        sum_signs(Head(i, jj - 4))
                    if h.j == 3:
                        sum_signs(Head(i, jj - 3))

            bodies(dve, body, first=2)
            sum_signs(Head(B - 1, 6))
            stats2(GROUPS - 2, 0)
            invert(GROUPS - 1)
            stats2(GROUPS - 1, 1)

        @block.gpsimd
        def _(pool):
            pool.memset(vt[:, :, :, :, HD:2 * HD], 0.0)
            pool.memset(vt[:, :, :, :, 3 * HD:4 * HD], 0.0)
            pool.memset(vt[:, :, :, :, 5 * HD:6 * HD], 0.0)
            pool.memset(vt[:, :, :, :, 2 * HD:3 * HD], 1.0)
            pool.memset(halves[:, 0:1], -0.5)
            pool.memset(halves[:, 1:2], 0.5)
            pool.memset(ytile[:, L + 2:YROW], 0.0)
            pool.memset(vt[:, :, :, :, 6 * HD:7 * HD], 1.0).then_inc(setup_pool, 1)
            pool.wait_ge(setup_pool, 1)

            def ln1(g):
                if not ok(g):
                    return
                s = LN1_STEPS * g
                wait(pool, kmax_ready, g + 1)
                settle(pool)
                pool.partition_all_reduce(small[:, 1:2], small[:, 0:1], P, ABSMAX).then_inc(kmax_all, 1)
                wait(pool, moments_ready, g + 1)
                settle(pool)
                pool.tensor_scalar(sml[:, 0:1], mv[:, 1:2], LN_EPS, None, ALU.add).then_inc(ln1_step, 1)
                wait(pool, ln1_step, s + 1)
                pool.tensor_tensor(sml[:, 1:2], sml[:, 0:1], halves[:, 0:1], ALU.pow).then_inc(ln1_step, 1)
                wait(pool, ln1_step, s + 2)
                settle(pool)
                pool.tensor_scalar(sml[:, 2:3], sml[:, 1:2], Q_SCALE, None, ALU.mult).then_inc(ln1_step, 1)
                wait(pool, ln1_step, s + 3)
                pool.tensor_tensor(sml[:, 4:5], mv[:, 0:1], sml[:, 2:3], ALU.mult).then_inc(ln1_step, 1)
                wait(pool, ln1_step, s + 4)
                settle(pool)
                pool.tensor_scalar(sml[:, 3:4], sml[:, 4:5], -1.0, None, ALU.mult).then_inc(ln1_step, 1)

            def residual(g, par):
                if not ok(g):
                    return
                wait(pool, rden_in, 16 * g + 16)
                pool.tensor_tensor(att[:, par], att[:, par], rden[:, par], ALU.mult).then_inc(ratio_done, 1)
                wait(pool, ratio_done, g + 1)
                wait(pool, xres_in, 16 * g + 16)
                pool.tensor_tensor(att[:, par], att[:, par], xres[:, par], ALU.add).then_inc(x2_done, 1)

            def ln2(g):
                if not ok(g):
                    return
                steps = [0]

                def step(ins):
                    steps[0] += 1
                    ins.then_inc(ln2_step, 1)
                    wait(pool, ln2_step, LN2_STEPS * g + steps[0])
                    settle(pool)

                wait(pool, moments2_ready, g + 1)
                wait(pool, y_done, g)
                settle(pool)
                c = [sm2[:, k:k + 1] for k in range(12)]
                step(pool.tensor_scalar(c[0], mv2[:, 1:2], LN_EPS, None, ALU.add))
                step(pool.tensor_tensor(c[1], c[0], halves[:, 0:1], ALU.pow))
                step(pool.tensor_tensor(c[2], c[0], halves[:, 1:2], ALU.pow))
                step(pool.tensor_tensor(c[3], c[1], c[1], ALU.mult))
                step(pool.tensor_tensor(c[3], c[3], mv2[:, 1:2], ALU.mult))
                step(pool.tensor_scalar(c[3], c[3], RMS_EPS, None, ALU.add))
                step(pool.tensor_tensor(c[4], c[3], halves[:, 0:1], ALU.pow))
                step(pool.tensor_tensor(c[5], c[3], halves[:, 1:2], ALU.pow))
                step(pool.tensor_tensor(c[6], c[1], c[4], ALU.mult))
                step(pool.tensor_tensor(c[8], c[6], mv2[:, 0:1], ALU.mult))
                step(pool.tensor_scalar(c[7], c[8], -1.0, None, ALU.mult))
                wait(pool, y_out, 16 * g)
                settle(pool)
                step(pool.tensor_scalar(ytile[:, L:L + 1], c[2], 1.0, c[5], ALU.add, ALU.mult))
                step(pool.tensor_copy(ytile[:, L + 1:L + 2], mv2[:, 0:1]))

            ln1(0)
            ln1(1)

            def body(i):
                for par in range(2):
                    g = 2 * i + par
                    ln1(g + 2)
                    ln2(g - 2)
                    residual(g - 1, 1 - par)

            bodies(pool, body, first=2)
            ln2(GROUPS - 2)
            residual(GROUPS - 1, 1)
            ln2(GROUPS - 1)

        attention.close()
        block = stack.enter_context(nc.Block())

        def passes(eng, body, n, first=1, last=1):
            for i in range(first):
                body(i)
            with eng.Fori(first, n - last) as i:
                body(i)
            for i in range(n - last, n):
                body(i)

        class Tile:

            def __init__(self, i, jj, count=TILES, per_pass=4):
                self.n, self.par, self.slot = per_pass * i + jj, jj % 2, jj % per_pass
                self.turn = per_pass // 2 * i + jj // 2
                self.slot_turn = i + jj // per_pass
                self.exists = not isinstance(i, int) or 0 <= self.n < count

        def registers(eng, name):
            return [[eng.alloc_register(f"{name}{par}{b}") for b in range(TB)] for par in range(2)]

        def load_experts(eng, regs, tile):
            settle(eng)
            eng.load(regs[tile.par], expert_of[0:1, bass.ds(TB * tile.n, TB)])

        def expert(eng, regs, tile, b):
            return eng.snap(regs[tile.par][b], min_val=0, max_val=EXPERTS - 1)

        @block.sync
        def _(sp):
            sp.dma_start(cst, cst_h).then_inc(cst_in, 16)
            sp.dma_start(ds_sb[0:EXPERTS], ds_h).then_inc(scale_in, 16)
            sp.dma_start(os_sb[0:EXPERTS], os_h).then_inc(scale_in, 16)

            sp_regs = registers(sp, "sp_expert")

            def load_rows(tile):
                if not tile.exists:
                    return
                g, par = tile.n, tile.par
                wait(sp, tok_t, g - 3)
                sp.dma_start(rows[:, tile.slot], ytab[bass.ds(g, 1)].rearrange("a p q -> (a p) q"))\
                    .then_inc(row_in[tile.slot], 16)

            def load_scales(tile):
                t, par = tile.n, tile.par
                wait(sp, prod_ready, t - 1)
                load_experts(sp, sp_regs, tile)
                for b in range(TB):
                    e = expert(sp, sp_regs, tile, b)
                    sp.dma_start(scl[b * BLK:(b + 1) * BLK, par],
                                 sctab[bass.ds(e, 1), :].broadcast_to([BLK, L])).then_inc(scl_in[par], 16)

            def body_rows(i):
                for k in range(4):
                    load_rows(Tile(i, k, GROUPS))

            def body_scales(i):
                for k in range(4):
                    load_scales(Tile(i, k))

            passes(sp, body_rows, GROUPS // 4)
            sp.wait_ge(sctab_ready, 1)
            sp.dma_start(sctab, scale_sb[0:EXPERTS]).then_inc(sctab_out, 16)
            sp.wait_ge(sctab_out, 16)
            sp.wait_ge(expert_ready, 1)
            passes(sp, body_scales, TILES // 4)

        @block.tensor
        def _(pe):
            t_ps = [st_ps[:, k, :].rearrange("p (c n) -> p c n", c=KC) for k in range(2)]
            h_ps = [st_ps[:, k, 0:2 * P].rearrange("p (b k n) -> p b k n", b=TB, k=2) for k in (2, 3)]
            pe_regs = registers(pe, "pe_expert")

            def turn_rows(tile):
                if not tile.exists:
                    return
                g, par = tile.n, tile.par
                wait(pe, row_in[tile.slot], 16 * tile.slot_turn + 16)
                wait(pe, xt_ready, g - 1)
                for c in range(KC):
                    mm = pe.transpose(t_ps[par][:, c, :], rows[:, tile.slot, c * P:(c + 1) * P], ident)
                mm.then_inc(tok_t, 1)

            def scores(tile):
                g, par = tile.n, tile.par
                wait(pe, xt_ready, g + 1)
                wait(pe, score_copied, g - 1)
                for c in range(KC):
                    mm = pe.matmul(banks[par][:, 0:EXPERTS + CLUSTERS], xt[:, par, c], sigw[:, c],
                                   start=(c == 0), stop=(c == KC - 1))
                mm.then_inc(score_done, 1)

            def body_scores(i):
                for k in range(4):
                    turn_rows(Tile(i, k + 1, GROUPS))
                    if k == 0 and isinstance(i, int) and i == 0:
                        pe.wait_ge(sig_ready, 1)
                    scores(Tile(i, k, GROUPS))

            pe.wait_ge(cst_in, 16)
            turn_rows(Tile(0, 0, GROUPS))
            passes(pe, body_scores, GROUPS // 4)

            pe.wait_ge(onehot_ready, GROUPS // 4)
            flat = onehot[:, :, :].rearrange("p g e -> p (g e)")
            for g in range(GROUPS):
                mm = pe.matmul(banks[2][0:EXPERTS, 0:P], onehot[:, g, :], ones16,
                               start=(g == 0), stop=(g == GROUPS - 1))
            mm.then_inc(count_done, 1)
            for half in range(2):
                cols = slice(half * L, (half + 1) * L)
                pe.matmul(st_ps[:, half, :], tri16, flat[:, cols], start=True, stop=True)
                mm = pe.matmul(st_ps[:, 2 + half, :], ones16, flat[:, cols], start=True, stop=True)
            mm.then_inc(rank_done, 1)
            pe.wait_ge(nblk_ready, 1)
            pe.matmul(banks[0][:, 0:EXPERTS], nblk[0:EXPERTS], tri16[0:EXPERTS, 0:EXPERTS],
                      start=True, stop=True)
            pe.matmul(banks[1][0:EXPERTS, 0:P], tri16[0:EXPERTS, 0:EXPERTS], nblk[0:EXPERTS],
                      start=True, stop=True).then_inc(start_done, 1)
            pe.wait_ge(ended_ready, 1)
            pe.matmul(banks[3][:, 0:BLOCKS], ones16[0:EXPERTS], ended[0:EXPERTS],
                      start=True, stop=True).then_inc(expert_done, 1)
            pe.wait_ge(live_ready, 1)
            pe.matmul(banks[1][:, 0:BLOCKS], us[0:EXPERTS], live[0:EXPERTS],
                      start=True, stop=True).then_inc(us_done, 1)
            pe.wait_ge(slots_ready, 1)
            for g in range(GROUPS):
                mm = pe.matmul(banks[2][:, 0:TILES], slot_p[:, g], slot_a[:, g],
                               start=(g == 0), stop=(g == GROUPS - 1))
            mm.then_inc(list_done, 1)

            def turn_slots(tile):
                if not tile.exists:
                    return
                t, par = tile.n, tile.par
                wait(pe, gathered[tile.slot], 16 * tile.slot_turn + 16)
                wait(pe, xlo_ready, t - 1)
                for c in range(KC):
                    mm = pe.transpose(t_ps[par][:, c, :], rows[:, tile.slot, c * P:(c + 1) * P], ident)
                mm.then_inc(slot_t, 1)

            def up(tile, b):
                e = expert(pe, pe_regs, tile, b)
                cols = slice(b * BLK, (b + 1) * BLK)
                for c in range(KC):
                    w = w_up[:, c, bass.ds(e, 1), :].rearrange("p a h -> p (a h)")
                    mm = pe.matmul(h_ps[tile.par][:, b], w, xhl[:, tile.par, :, c, cols],
                                   start=(c == 0), stop=(c == KC - 1))
                if b == TB - 1:
                    mm.then_inc(up_done, 1)

            def down(tile, b):
                if not tile.exists:
                    return
                e = expert(pe, pe_regs, tile, b)
                w = w_dn[:, bass.ds(e, 1), :].rearrange("p a n -> p (a n)")
                for k in range(2):
                    mm = pe.matmul(banks[tile.par], hz[:, tile.par, k, b * P:(b + 1) * P], w,
                                   start=(b == 0 and k == 0), stop=(b == TB - 1 and k == 1))
                if b == TB - 1:
                    mm.then_inc(down_done, 1)

            def await_up(tile):
                wait(pe, xlo_ready, tile.n + 1)
                wait(pe, hid_ready, tile.n - 1)
                load_experts(pe, pe_regs, tile)

            def await_down(tile):
                if not tile.exists:
                    return
                wait(pe, hlo_ready, tile.n + 1)
                wait(pe, prod_ready, tile.n - 1)

            def body_slots(i):
                for k in range(4):
                    turn_slots(Tile(i, k + 1))
                    await_up(Tile(i, k))
                    for b in range(TB):
                        up(Tile(i, k), b)
                        if b == 0:
                            await_down(Tile(i, k - 1))
                        down(Tile(i, k - 1), b)

            pe.wait_ge(expert_ready, 1)
            turn_slots(Tile(0, 0))
            passes(pe, body_slots, TILES // 4)
            await_down(Tile(TILES // 4 - 1, 3))
            for b in range(TB):
                down(Tile(TILES // 4 - 1, 3), b)

        @block.scalar
        def _(act):
            sums = sums_h[:, :].rearrange("p (c e) -> p c e", c=KC)
            act.activation(sigw[:, :, 0:EXPERTS], sums, ACT.Sign).then_inc(sig_tiles, 1)
            act.wait_ge(csum_ready, 1)
            act.activation(sigw[:, :, EXPERTS:], csum[:, :, :], ACT.Sign).then_inc(sig_clusters, 1)

            def copy_xt(tile):
                if not tile.exists:
                    return
                g, par = tile.n, tile.par
                wait(act, tok_t, g + 1)
                wait(act, score_done, g - 1)
                act.activation(xt[:, par].rearrange("p c n -> p (c n)"), st_ps[:, par, :], ACT.Copy)\
                    .then_inc(xt_ready, 1)

            def body_rows(i):
                for k in range(4):
                    copy_xt(Tile(i, k, GROUPS))

            passes(act, body_rows, GROUPS // 4)

            def split_high(tile):
                if not tile.exists:
                    return
                t, par = tile.n, tile.par
                wait(act, slot_t, t + 1)
                wait(act, up_done, t - 1)
                for c in range(KC):
                    ins = act.activation(xhl[:, par, 0, c], st_ps[:, par, c * P:(c + 1) * P], ACT.Copy,
                                         scale=wn[:, c:c + 1])
                ins.then_inc(xhi_ready, 1)

            def residual(tile):
                t, par = tile.n, tile.par
                wait(act, gathered[tile.slot], 16 * tile.slot_turn + 16)
                wait(act, res_ready, t - 1)
                act.activation(base[:, par], rows[:, tile.slot, 0:L], ACT.Identity,
                               bias=rows[:, tile.slot, L + 1:L + 2], scale=rows[:, tile.slot, L:L + 1])\
                    .then_inc(base_ready, 1)

            def body_slots(i):
                for k in range(4):
                    split_high(Tile(i, k + 1))
                    residual(Tile(i, k))

            split_high(Tile(0, 0))
            passes(act, body_slots, TILES // 4)

        @block.vector
        def _(dve):
            n = [0]

            def step(ins):
                n[0] += 1
                ins.then_inc(ffn_step, 1)
                dve.wait_ge(ffn_step, n[0])

            sigs = sigw[:, :, :]
            dve.tensor_reduce(mags[:, 0:1], wn[:, :], AX.X, ALU.max, apply_absolute_value=True)\
                .then_inc(mags_ready, 1)
            step(dve.memset(mags[:, 1:2], 0.0))
            dve.tensor_reduce(mags[0:EXPERTS, 1:2], us[0:EXPERTS], AX.X, ALU.max,
                              apply_absolute_value=True)\
                .then_inc(mags_ready, 1)
            dve.wait_ge(sig_tiles, 1)
            dve.tensor_reduce(csum[:, :, :], sigs[:, :, 0:EXPERTS].rearrange(
                "p c (a b) -> p c a b", b=EXPERTS // CLUSTERS), AX.X, ALU.add).then_inc(csum_ready, 1)
            dve.wait_ge(mags_all, 1)
            step(dve.tensor_scalar(powers[:, 0:2], mags[:, 2:4], 2.0 ** -60, None, ALU.max))
            step(dve.tensor_scalar(powers[:, 2:4].bitcast(I32), powers[:, 0:2].bitcast(I32), EXPO, None,
                                   ALU.bitwise_and))
            step(dve.tensor_scalar(powers[:, 4:6].bitcast(I32), powers[:, 2:4].bitcast(I32), -1.0,
                                   float(0x7F000000), ALU.mult, ALU.add))
            step(dve.tensor_scalar(wn[:, :], wn[:, :], powers[:, 4:5], X_SCALE, ALU.mult, ALU.mult))
            step(dve.tensor_scalar(us[0:EXPERTS], us[0:EXPERTS], powers[0:EXPERTS, 5:6], H_SCALE / X_SCALE,
                                   ALU.mult, ALU.mult))
            dve.wait_ge(sig_clusters, 1)
            dve.tensor_tensor(sigs, sigs, wn[:, :].unsqueeze(2).to_broadcast(
                [P, KC, EXPERTS + CLUSTERS]), ALU.mult).then_inc(sig_ready, 1)
            step(dve.tensor_scalar(powers[:, 0:1], powers[:, 2:3], powers[:, 3:4], 1.0 / H_SCALE,
                                   ALU.mult, ALU.mult))
            dve.wait_ge(scale_in, 32)
            dve.tensor_scalar(scale_sb[0:EXPERTS], ds_sb[0:EXPERTS], os_sb[0:EXPERTS, 0:1],
                              powers[0:EXPERTS, 0:1], ALU.mult, ALU.mult).then_inc(sctab_ready, 1)
            dve.wait_ge(cst_in, 16)
            dve.tensor_copy(tri16, cst[:, C_TRI:C_TRI + P])
            dve.memset(ones16, 1.0)

            def copy_scores(tile):
                g, par = tile.n, tile.par
                wait(dve, score_done, g + 1)
                dve.tensor_copy(score[:, tile.slot], banks[par][:, 0:EXPERTS + CLUSTERS])\
                    .then_inc(score_copied, 1)

            def per_tile(col, width, tiles=GROUPS):
                return col.unsqueeze(2).to_broadcast([P, tiles, width])

            def per_expert(c0, width, tiles=GROUPS):
                return cst[:, c0:c0 + width].unsqueeze(1).to_broadcast([P, tiles, width])

            top, first, ttop, expert_no = pick

            def route(i):
                done = [0]

                def route_step(ins):
                    done[0] += 1
                    ins.then_inc(routed, 1)
                    wait(dve, routed, 10 * i + done[0])

                a, b = near[:, 0], near[:, 1]
                tiles_s, clusters_s = score[:, :, 0:EXPERTS], score[:, :, EXPERTS:]
                wait(dve, score_copied, 4 * i + 4)
                route_step(dve.tensor_reduce(top, clusters_s, AX.X, ALU.max))
                route_step(dve.tensor_tensor(ckey, clusters_s, per_tile(top, CLUSTERS, 4), ALU.is_lt))
                route_step(dve.scalar_tensor_tensor(ckey, ckey, 64.0, per_expert(C_CL8, CLUSTERS, 4),
                                                    ALU.mult, ALU.add))
                route_step(dve.tensor_reduce(first, ckey, AX.X, ALU.min))
                route_step(dve.tensor_tensor(a, per_expert(C_CL64, EXPERTS, 4),
                                             per_tile(first, EXPERTS, 4), ALU.not_equal))
                route_step(dve.scalar_tensor_tensor(b, a, -3e38, tiles_s, ALU.mult, ALU.add))
                route_step(dve.tensor_reduce(ttop, b, AX.X, ALU.max))
                route_step(dve.tensor_tensor(a, b, per_tile(ttop, EXPERTS, 4), ALU.is_lt))
                route_step(dve.scalar_tensor_tensor(b, a, 128.0, per_expert(C_E64, EXPERTS, 4),
                                                    ALU.mult, ALU.add))
                route_step(dve.tensor_reduce(expert_no, b, AX.X, ALU.min))
                dve.tensor_tensor(onehot[:, bass.ds(4 * i, 4), :], per_expert(C_E64, EXPERTS, 4),
                                  per_tile(expert_no, EXPERTS, 4), ALU.is_equal)\
                    .then_inc(onehot_ready, 1)

            def body_scores(i):
                for k in range(4):
                    copy_scores(Tile(i, k, GROUPS))
                route(i)

            passes(dve, body_scores, GROUPS // 4)
            a, b = work

            dve.wait_ge(count_done, 1)
            step(dve.tensor_scalar(counts_i[0:EXPERTS], banks[2][0:EXPERTS, 0:P], float(BLK - 1), None,
                                   ALU.add))
            step(dve.tensor_scalar(counts_i[0:EXPERTS], counts_i[0:EXPERTS], int(math.log2(BLK)), None,
                                   ALU.arith_shift_right))
            dve.tensor_copy(nblk[0:EXPERTS], counts_i[0:EXPERTS]).then_inc(nblk_ready, 1)
            dve.wait_ge(start_done, 1)
            step(dve.tensor_scalar(before[:, 0, :], banks[0][:, 0:EXPERTS], float(BLK), None, ALU.mult))
            dve.wait_ge(nblk_ready, 1)
            step(dve.tensor_tensor(ends[0:EXPERTS], banks[1][0:EXPERTS, 0:P], nblk[0:EXPERTS], ALU.add))
            block_no = cst[0:EXPERTS, C_ROWP:C_ROWP + P]
            step(dve.tensor_tensor(ended[0:EXPERTS], ends[0:EXPERTS], block_no, ALU.is_le))
            dve.tensor_tensor(live[0:EXPERTS], banks[1][0:EXPERTS, 0:P], block_no, ALU.is_le)\
                .then_inc(ended_ready, 1)
            dve.wait_ge(ended_ready, 1)
            dve.tensor_tensor(live[0:EXPERTS], live[0:EXPERTS], ended[0:EXPERTS], ALU.subtract)\
                .then_inc(live_ready, 1)
            dve.wait_ge(rank_done, 1)
            for g in range(1, GROUPS):
                k = g - 1
                step(dve.tensor_tensor(before[:, g, :], before[:, k, :],
                                       st_ps[:, 2 + k // 8, (k % 8) * EXPERTS:(k % 8 + 1) * EXPERTS],
                                       ALU.add))
            dve.wait_ge(expert_done, 1)
            dve.tensor_scalar(expert_of, banks[3][:, 0:BLOCKS], float(EXPERTS - 1), None, ALU.min)\
                .then_inc(expert_ready, 1)
            dve.wait_ge(us_done, 1)
            step(dve.tensor_copy(us_of, banks[1][:, 0:BLOCKS]))
            ranks = st_ps[:, 0:2, :].rearrange("p c (g e) -> p (c g) e", e=EXPERTS)
            step(dve.tensor_tensor(a, before, ranks, ALU.add))
            step(dve.tensor_tensor(b, a, onehot, ALU.mult))
            step(dve.tensor_reduce(slot_f, b, AX.X, ALU.add))
            step(dve.tensor_copy(slot_i[:, 0], slot_f))
            step(dve.tensor_scalar(slot_i[:, 1], slot_i[:, 0], P - 1, None, ALU.bitwise_and))
            step(dve.tensor_scalar(slot_i[:, 2], slot_i[:, 0], int(math.log2(P)), None,
                                   ALU.arith_shift_right))
            step(dve.tensor_copy(lo_f, slot_i[:, 1]))
            step(dve.tensor_copy(hi_f, slot_i[:, 2]))
            step(dve.tensor_tensor(slot_p, per_expert(C_ROWP, P), per_tile(lo_f, P), ALU.is_equal))
            step(dve.tensor_tensor(slot_a, per_expert(C_A32, TILES), per_tile(hi_f, TILES),
                                   ALU.is_equal))
            dve.tensor_tensor(slot_a, slot_a, per_tile(cst[:, C_TOK:C_TOK + GROUPS], TILES), ALU.mult)\
                .then_inc(slots_ready, 1)
            dve.wait_ge(list_done, 1)
            step(dve.tensor_scalar(absent, banks[2][:, 0:TILES], 0.5, 1e6, ALU.is_lt, ALU.mult))
            dve.scalar_tensor_tensor(token_of, banks[2][:, 0:TILES], -1.0, absent, ALU.add, ALU.add)\
                .then_inc(list_ready, 1)

            def split_low(tile):
                if not tile.exists:
                    return
                t, par = tile.n, tile.par
                wait(dve, xhi_ready, t + 1)
                for c in range(KC):
                    ins = dve.scalar_tensor_tensor(xhl[:, par, 1, c], st_ps[:, par, c * P:(c + 1) * P],
                                                   wn[:, c:c + 1], xhl[:, par, 0, c], ALU.mult,
                                                   ALU.subtract)
                ins.then_inc(xlo_ready, 1)

            def hidden(tile):
                t, par = tile.n, tile.par
                wait(dve, up_done, t + 1)
                wait(dve, hlo_ready, t - 1)
                dve.tensor_tensor(
                    hparts[:, par], st_ps[:, 2 + par, 0:2 * P].rearrange("p (b n) -> p b n", b=TB),
                    us_of[:, bass.ds(TB * t, TB)].unsqueeze(2).to_broadcast([P, TB, 2 * BLK]),
                    ALU.mult).then_inc(hid_ready, 1)
                wait(dve, hid_ready, t + 1)
                src = hid[:, par].rearrange("p (b n) -> p b n", n=BLK)
                dve.tensor_tensor(src, hparts[:, par, :, 0:BLK], hparts[:, par, :, BLK:], ALU.add)\
                    .then_inc(hsum_ready, 1)
                high, low = [hz[:, par, k].rearrange("p (b n) -> p b n", n=P + BLK)[:, :, 0:BLK]
                             for k in range(2)]
                wait(dve, hsum_ready, t + 1)
                wait(dve, down_done, t - 1)
                settle(dve)
                dve.tensor_scalar(high, src, 0.0, None, ALU.max).then_inc(hhi_ready, 1)
                wait(dve, hhi_ready, t + 1)
                dve.scalar_tensor_tensor(low, src, 0.0, high, ALU.max, ALU.subtract)\
                    .then_inc(hlo_ready, 1)

            def scaled(tile):
                if not tile.exists:
                    return
                t, par = tile.n, tile.par
                wait(dve, down_done, t + 1)
                wait(dve, scl_in[par], 16 * TB * (tile.turn + 1))
                wait(dve, scattered[tile.slot], 16 * tile.slot_turn)
                dve.tensor_tensor(res[:, tile.slot], banks[par], scl[:, par], ALU.mult)\
                    .then_inc(prod_ready, 1)
                wait(dve, prod_ready, t + 1)
                wait(dve, base_ready, t + 1)
                dve.tensor_tensor(res[:, tile.slot], res[:, tile.slot], base[:, par], ALU.add)\
                    .then_inc(res_ready, 1)

            def body_slots(i):
                for k in range(4):
                    split_low(Tile(i, k + 1))
                    hidden(Tile(i, k))
                    scaled(Tile(i, k - 1))

            dve.wait_ge(clean, 2)
            dve.wait_ge(expert_ready, 1)
            split_low(Tile(0, 0))
            passes(dve, body_slots, TILES // 4, first=2)
            scaled(Tile(TILES // 4 - 1, 3))

        @block.gpsimd
        def _(pool):
            pool.wait_ge(mags_ready, 2)
            pool.partition_all_reduce(mags[:, 2:4], mags[:, 0:2], P, ABSMAX).then_inc(mags_all, 1)
            pool.memset(hz[:, 0], 0.0).then_inc(clean, 1)
            pool.memset(hz[:, 1], 0.0).then_inc(clean, 1)
            pool.wait_ge(tok_t, GROUPS)

            def gather(tile):
                if not tile.exists:
                    return
                t, k = tile.n, tile.slot
                wait(pool, slot_t, t - 3)
                wait(pool, base_ready, t - 3)
                settle(pool)
                pool.tensor_copy(gidx[:, k:k + 1], token_of[:, bass.ds(t, 1)]).then_inc(gidx_ready, 1)
                wait(pool, gidx_ready, t + 1)
                settle(pool)
                pool.indirect_dma_start(
                    rows[:, k], None, ytab.rearrange("g p n -> (g p) n"),
                    bass.IndirectOffsetOnAxis(ap=gidx[:, k:k + 1], axis=0),
                    bounds_check=TOKENS - 1, oob_is_err=False).then_inc(gathered[k], 16)

            def finish(tile):
                if not tile.exists:
                    return
                t, k = tile.n, tile.slot
                wait(pool, scattered[k], 16 * tile.slot_turn)
                settle(pool)
                pool.tensor_copy(sidx[:, k:k + 1], token_of[:, bass.ds(t, 1)]).then_inc(sidx_ready, 1)
                wait(pool, sidx_ready, t + 1)
                wait(pool, res_ready, t + 1)
                settle(pool)
                pool.indirect_dma_start(
                    out, bass.IndirectOffsetOnAxis(ap=sidx[:, k:k + 1], axis=0),
                    res[:, k], None, bounds_check=TOKENS - 1, oob_is_err=False)\
                    .then_inc(scattered[k], 16)

            def body_slots(i):
                for k in range(4):
                    gather(Tile(i, k + 3))
                    finish(Tile(i, k - 1))

            pool.wait_ge(list_ready, 1)
            for k in range(3):
                gather(Tile(0, k))
            passes(pool, body_slots, TILES // 4, first=2, last=1)
            finish(Tile(TILES // 4 - 1, 3))
            for k in range(4):
                pool.wait_ge(scattered[k], 16 * (TILES // 4))


_INS = ["x", "ctx_k", "ctx_v", "klen", "up_h", "dn_h", "us_h", "ds_h", "os_h", "w_h", "cst_h"]


def lay_out(i):
    import numpy as np

    a = {k: np.asarray(v) for k, v in i.items()}
    ctx = a["ctx_2048"]
    up, dn = a["L0_ffn_up_w"], a["L0_ffn_down_w"]
    return {
        "x": a["x"].reshape(GROUPS, P, L),
        "ctx_k": ctx.reshape(GROUPS, P, L),
        "ctx_v": ctx.reshape(GROUPS, 2, 2, HD, KC, P).transpose(0, 2, 5, 4, 1, 3).reshape(
            GROUPS, 2, P, KC * 2, HD),
        "klen": a["itok_B_779_1933"],
        "up_h": up.reshape(8, 8, HID, KC, P).transpose(3, 0, 4, 1, 2).reshape(NUP, P, CH),
        "dn_h": dn.reshape(NUP, 2, L, HID).transpose(0, 3, 1, 2).reshape(NUP, P, CH),
        "us_h": a["L0_ffn_up_scale"],
        "ds_h": a["L0_ffn_down_scale"],
        "os_h": a["L0_ffn_output_scale"].reshape(EXPERTS, 1),
        "w_h": a["L0_ffn_norm_weight"].reshape(KC, P).T,
        "cst_h": constants(),
    }


def kernel(**inputs):
    import numpy as np
    import concourse.bacc as bacc
    from concourse.bass_utils import run_bass_kernel_spmd

    nc = bacc.Bacc("TRN2", target_bir_lowering=False, num_devices=1)
    arrays, args = {}, []
    laid = lay_out(inputs)
    for name in _INS:
        arr = np.ascontiguousarray(laid[name])
        arrays[f"in_{name}"] = arr
        args.append(nc.dram_tensor(f"in_{name}", arr.shape, mybir.dt.from_np(arr.dtype),
                                   kind="ExternalInput").ap())
    out = nc.dram_tensor("out_0", (TOKENS, L), F32, kind="ExternalOutput").ap()
    split_d = nc.dram_tensor("split_d", (GROUPS, P, 4, L), F16, kind="Internal").ap()
    inv_d = nc.dram_tensor("inv_d", (GH, L), F32, kind="Internal").ap()
    ytab = nc.dram_tensor("ytab", (GROUPS, P, YROW), F32, kind="Internal").ap()
    sctab = nc.dram_tensor("sctab", (EXPERTS, L), F32, kind="Internal").ap()
    build(nc, *args, out, split_d, inv_d, ytab, sctab)
    res = run_bass_kernel_spmd(nc, [arrays], core_ids=[0])
    return res.results[0]["out_0"].reshape(B, C, L)
```

```python
import math
from contextlib import ExitStack

import concourse.bass as bass
from concourse import mybir

F32 = mybir.dt.float32
F16 = mybir.dt.float16
BF16 = mybir.dt.bfloat16
I32 = mybir.dt.int32
ALU = mybir.AluOpType
ACT = mybir.ActivationFunctionType
AX = mybir.AxisListType
ABSMAX = bass.bass_isa.ReduceOp.absmax

P = 128
B, C, L = 8, 256, 512
HD = 32
HEADS = B * C // HD
GROUPS = B * C // P
GH = P // HD
KC = L // P
EXPERTS, HID = 64, 128
CLUSTERS = 8
BLK = 32
BLOCKS = 128
TOKENS = GROUPS * P
TILES = BLOCKS * BLK // P
TB = P // BLK
CH = 1024
NUP = EXPERTS * HID * KC // CH
ATT_SCALE = 1.0 / (64 ** 0.5 * math.log(20))
LN_EPS, RMS_EPS = 1e-5, 1e-6
ARENA = 19480
EXPO = 0x7F800000
Q_SCALE = 8.0
K_SCALE = 4096.0
X_SCALE = 512.0
H_SCALE = 16.0
LN1_STEPS, LN2_STEPS = 5, 13
YROW = L + 4

C_TRI, C_ROWP = 0, P
C_E64 = C_ROWP + P
C_CL64 = C_E64 + EXPERTS
C_A32 = C_CL64 + EXPERTS
C_TOK = C_A32 + TILES
C_CL8 = C_TOK + GROUPS
C_END = C_CL8 + CLUSTERS


def constants():
    import numpy as np

    c = np.zeros((P, C_END), np.float32)
    p, r = np.arange(P)[:, None], np.arange(P)[None, :]
    c[:, C_TRI:C_TRI + P] = p < r
    c[:, C_ROWP:C_ROWP + P] = r
    c[:, C_E64:C_E64 + EXPERTS] = np.arange(EXPERTS)
    c[:, C_CL64:C_CL64 + EXPERTS] = np.arange(EXPERTS) // (EXPERTS // CLUSTERS)
    c[:, C_A32:C_A32 + TILES] = np.arange(TILES)
    c[:, C_TOK:C_TOK + GROUPS] = p + P * np.arange(GROUPS)[None, :] + 1
    c[:, C_CL8:C_CL8 + CLUSTERS] = np.arange(CLUSTERS)
    return c


def build(nc, x, ctx_k, ctx_v, klen, up_h, dn_h, us_h, ds_h, os_h, w_h, ident_h, cst_h, out,
          split_d, inv_d, ytab, sctab):
    stack = ExitStack()
    with stack:
        def sb(name, shape, dt):
            return stack.enter_context(nc.sbuf_tensor(name, shape, dt))

        def sem(name):
            return stack.enter_context(nc.semaphore(name))

        w_up = sb("w_up", [P, KC, EXPERTS, HID], BF16)
        w_dn = sb("w_dn", [P, EXPERTS, L], BF16)
        ident = sb("ident", [P, P], F32)
        ident16 = sb("ident16", [P, P], F16)
        sums_h = sb("sums_h", [P, KC * EXPERTS], F32)
        expscale = sb("expscale", [P, GROUPS], F32)
        mags = sb("mags", [P, 4], F32)
        powers = sb("powers", [P, 6], F32)
        small = sb("small", [P, 4], F32)
        us = sb("us", [P, HID], F32)
        wn = sb("wn", [P, KC], F32)

        arena = sb("arena", [P, ARENA], F32)
        used = [0, 0]

        def carve(phase, words):
            a = used[phase]
            used[phase] += words
            assert used[phase] <= ARENA, used
            return arena[:, a:a + words]

        stage = carve(0, 2 * CH).rearrange("p (s n) -> p s n", s=2)
        pt = carve(0, 2 * KC * L).rearrange("p (s c q) -> p s c q", s=2, c=KC)
        qst = carve(0, 2 * GH * L // 2).bitcast(F16).rearrange("p (g j q) -> p g j q", g=2, j=GH)
        kst = carve(0, 2 * GH * L // 2).bitcast(F16).rearrange("p (g j q) -> p g j q", g=2, j=GH)
        vt = carve(0, 2 * KC * 2 * 7 * HD).rearrange("p (g c k n) -> p g c k n", g=2, c=KC, k=2)
        xin = carve(0, L)
        kin = carve(0, L)
        parts = carve(0, 4 * L // 2).bitcast(F16).rearrange("p (s q) -> p s q", s=4)
        xres = carve(0, 2 * L).rearrange("p (s q) -> p s q", s=2)
        att = carve(0, 2 * L).rearrange("p (s q) -> p s q", s=2)
        rden = carve(0, 2 * L).rearrange("p (s q) -> p s q", s=2)
        ytile = carve(0, YROW)
        dcol = carve(0, GH * L // P)
        mx = sb("mx", [P, 2, KC], F32)
        mhl = sb("mhl", [P, 2, KC, 2], F16)
        stat = sb("stat", [P, 6], F32)
        mv = sb("mv", [P, 2], F32)
        stat2 = sb("stat2", [P, 6], F32)
        mv2 = sb("mv2", [P, 2], F32)
        sml = sb("sml", [P, 16], F32)
        sm2 = sb("sm2", [P, 16], F32)
        kpow = sb("kpow", [P, 4], F32)
        halves = sb("halves", [P, 2], F32)
        lnk = sb("lnk", [P, B], F32)
        klen_i = sb("klen_i", [P, B], I32)

        cst = carve(1, C_END)
        rows = carve(1, 4 * YROW).rearrange("p (s n) -> p s n", s=4)
        sigw = carve(1, KC * (EXPERTS + CLUSTERS)).rearrange("p (c e) -> p c e", c=KC)
        csum = carve(1, KC * CLUSTERS).rearrange("p (c e) -> p c e", c=KC)
        ds_sb = carve(1, L)
        os_sb = carve(1, 1)
        scale_sb = carve(1, L)
        xt = carve(1, 2 * L).rearrange("p (s c n) -> p s c n", s=2, c=KC)
        score = carve(1, 4 * (EXPERTS + CLUSTERS)).rearrange("p (g e) -> p g e", g=4)
        near = carve(1, 8 * EXPERTS).rearrange("p (k g e) -> p k g e", k=2, g=4)
        ckey = carve(1, 4 * CLUSTERS).rearrange("p (g e) -> p g e", g=4)
        onehot = carve(1, GROUPS * EXPERTS // 2).bitcast(F16).rearrange("p (g e) -> p g e", g=GROUPS)
        pick = [carve(1, 4) for _ in range(4)]
        counts = carve(1, P)
        slot_f = carve(1, GROUPS)
        counts_i = carve(1, P).bitcast(I32)
        nblk = carve(1, P // 2).bitcast(F16)
        ends = carve(1, P)
        ended = carve(1, P // 2).bitcast(F16)
        slot_i = carve(1, 3 * GROUPS).bitcast(I32).rearrange("p (k g) -> p k g", k=3)
        slot_p = carve(1, GROUPS * P // 2).bitcast(F16).rearrange("p (g n) -> p g n", g=GROUPS)
        slot_a = carve(1, GROUPS * TILES // 2).bitcast(F16).rearrange("p (g n) -> p g n", g=GROUPS)
        tri16 = carve(1, P // 2).bitcast(F16)
        early_f = carve(1, EXPERTS)
        early = carve(1, EXPERTS // 2).bitcast(F16)
        tri_blk = carve(1, EXPERTS // 2).bitcast(F16)
        ones16 = carve(1, P // 2).bitcast(F16)
        absent = carve(1, TILES)
        token_of = carve(1, TILES).bitcast(I32)
        expert_of = carve(1, BLOCKS).bitcast(I32)
        gidx = carve(1, 4).bitcast(I32)
        sidx = carve(1, 4).bitcast(I32)
        xhl = carve(1, 2 * L).bitcast(F16).rearrange("p (s h c n) -> p s h c n", s=2, h=2, c=KC)
        hparts = carve(1, 4 * P).rearrange("p (s b n) -> p s b n", s=2, b=TB)
        hid = carve(1, 2 * P).rearrange("p (s b n) -> p s b n", s=2, b=TB)
        DIAG = TB * (P + BLK)
        hz = carve(1, 2 * DIAG).bitcast(F16).rearrange("p (s h n) -> p s h n", s=2, h=2)
        scl = carve(1, 2 * L).rearrange("p (s n) -> p s n", s=2)
        base = carve(1, 2 * L).rearrange("p (s n) -> p s n", s=2)
        res = carve(1, 4 * L).rearrange("p (s n) -> p s n", s=4)
        mine = res.rearrange("p s n -> p (s n)")[:, 0:GROUPS * EXPERTS].rearrange(
            "p (g e) -> p g e", g=GROUPS)
        live = carve(1, P)
        us_of = carve(1, BLOCKS)

        sq_ps = stack.enter_context(nc.psum_tensor("sq_ps", [P, 2, L], F32))
        pv_ps = stack.enter_context(nc.psum_tensor("pv_ps", [P, L], F32))
        mt_ps = stack.enter_context(nc.psum_tensor("mt_ps", [P, L], F32))
        st_ps = stack.enter_context(nc.psum_tensor("st_ps", [P, 4, L], F32))
        banks = [sq_ps[:, 0, :], sq_ps[:, 1, :], pv_ps[:, :], mt_ps[:, :]]

        const_in = sem("const_in")
        setup_dve = sem("setup_dve")
        setup_pool = sem("setup_pool")
        setup_steps = sem("setup_steps")
        lnk_ready = sem("lnk_ready")
        consts_ready = sem("consts_ready")
        sctab_out = sem("sctab_out")
        xk_in = sem("xk_in")
        v_in = sem("v_in")
        xres_in = sem("xres_in")
        stats_ready = sem("stats_ready")
        moments_ready = sem("moments_ready")
        kmax_ready = sem("kmax_ready")
        kmax_all = sem("kmax_all")
        ln1_step = sem("ln1_step")
        kpow_step = sem("kpow_step")
        q_ready = sem("q_ready")
        hi_ready = sem("hi_ready")
        parts_ready = sem("parts_ready")
        split_out = sem("split_out")
        stack_in = sem("stack_in")
        sq_done = sem("sq_done")
        max_done = sem("max_done")
        mhi_done = sem("mhi_done")
        mneg_done = sem("mneg_done")
        mrow_done = sem("mrow_done")
        mrow_copied = sem("mrow_copied")
        st_done = sem("st_done")
        exp_done = sem("exp_done")
        pv_done = sem("pv_done")
        dcol_in = sem("dcol_in")
        inverted = sem("inverted")
        inv_out = sem("inv_out")
        rden_in = sem("rden_in")
        att_evac = sem("att_evac")
        ratio_done = sem("ratio_done")
        x2_done = sem("x2_done")
        stats2_ready = sem("stats2_ready")
        moments2_ready = sem("moments2_ready")
        ln2_step = sem("ln2_step")
        y_done = sem("y_done")
        y_out = sem("y_out")
        w_in = [sem("w_in0"), sem("w_in1")]
        sign_done = sem("sign_done")
        sums_done = sem("sums_done")

        scale_in = sem("scale_in")
        mags_ready = sem("mags_ready")
        mags_all = sem("mags_all")
        ffn_step = sem("ffn_step")
        sig_tiles = sem("sig_tiles")
        csum_ready = sem("csum_ready")
        sig_clusters = sem("sig_clusters")
        sig_ready = sem("sig_ready")
        sctab_ready = sem("sctab_ready")
        row_in = [sem(f"row_in{k}") for k in range(4)]
        tok_t = sem("tok_t")
        xt_ready = sem("xt_ready")
        score_done = sem("score_done")
        score_copied = sem("score_copied")
        onehot_ready = sem("onehot_ready")
        rank_done = sem("rank_done")
        count_done = sem("count_done")
        nblk_ready = sem("nblk_ready")
        start_done = sem("start_done")
        ended_ready = sem("ended_ready")
        expert_done = sem("expert_done")
        expert_ready = sem("expert_ready")
        slots_ready = sem("slots_ready")
        list_done = sem("list_done")
        list_ready = sem("list_ready")
        clean = sem("clean")
        gidx_ready = sem("gidx_ready")
        sidx_ready = sem("sidx_ready")
        gathered = [sem(f"gathered{k}") for k in range(4)]
        slot_t = sem("slot_t")
        xhi_ready = sem("xhi_ready")
        xlo_ready = sem("xlo_ready")
        up_done = sem("up_done")
        live_ready = sem("live_ready")
        us_done = sem("us_done")
        hid_ready = sem("hid_ready")
        hhi_ready = sem("hhi_ready")
        hlo_ready = sem("hlo_ready")
        down_done = sem("down_done")
        scl_in = [sem("scl_in0"), sem("scl_in1")]
        base_ready = sem("base_ready")
        prod_ready = sem("prod_ready")
        res_ready = sem("res_ready")
        scattered = [sem(f"scattered{k}") for k in range(4)]
        cst_in = sem("cst_in")
        routed = sem("routed")
        hsum_ready = sem("hsum_ready")
        slot_low = sem("slot_low")
        slot_high = sem("slot_high")
        numbered = sem("numbered")

        def wait(eng, s, v):
            if not (isinstance(v, int) and v <= 0):
                eng.wait_ge(s, v)

        class Head:

            def __init__(self, i, jj):
                self.n, self.j, self.slot = 8 * i + jj, jj % GH, jj % 2
                self.g, self.par = 2 * i + jj // GH, jj // GH % 2
                self.pair = 4 * i + jj // 2
                self.exists = not isinstance(i, int) or 0 <= self.n < HEADS

        def settle(eng):
            eng.sem_inc(settled[eng.engine], 1)

        def ok(g):
            return not isinstance(g, int) or 0 <= g < GROUPS

        def bodies(eng, body, first=1, last=1):
            for i in range(first):
                body(i)
            with eng.Fori(first, B - last) as i:
                body(i)
            for i in range(B - last, B):
                body(i)

        settled = {e.engine: sem(f"settled{k}") for k, e in enumerate(
            (nc.scalar, nc.vector, nc.gpsimd, nc.sync, nc.tensor))}
        def collect_den(sp, g, par):
            if not ok(g):
                return
            wait(sp, att_evac, 2 * g + 2)
            sp.dma_start(dcol, rden[0:P:HD, par, :]).then_inc(dcol_in, 16)

        def spread_inverses(sp, g, par):
            if not ok(g):
                return
            wait(sp, inverted, g + 1)
            sp.dma_start(inv_d.rearrange("j (k c) -> (j k) c", c=GH * L // P), dcol)\
                .then_inc(inv_out, 16)
            wait(sp, inv_out, 16 * g + 16)
            sp.dma_start(rden[:, par, :], bass.AP(inv_d.tensor, 0, [[L, GH], [0, HD], [1, L]]))\
                .then_inc(rden_in, 16)

        def put_y(sp, g):
            if not ok(g):
                return
            wait(sp, y_done, g + 1)
            sp.dma_start(ytab[bass.ds(g, 1)].rearrange("a p q -> (a p) q"), ytile)\
                .then_inc(y_out, 16)

        def norm_y(act, g, par):
            if not ok(g):
                return
            wait(act, ln2_step, LN2_STEPS * g + LN2_STEPS)
            act.activation(ytile[:, 0:L], att[:, par], ACT.Identity, bias=sm2[:, 7:8],
                           scale=sm2[:, 6:7]).then_inc(y_done, 1)

        def invert(dve, g):
            if not ok(g):
                return
            wait(dve, dcol_in, 16 * g + 16)
            dve.reciprocal(dcol, dcol).then_inc(inverted, 1)

        def stats2(dve, g, par):
            if not ok(g):
                return
            wait(dve, x2_done, g + 1)
            dve.bn_stats(stat2[:, :], att[:, par]).then_inc(stats2_ready, 1)
            wait(dve, stats2_ready, g + 1)
            wait(dve, ln2_step, LN2_STEPS * g)
            settle(dve)
            dve.bn_aggr(mv2[:, :], stat2[:, :]).then_inc(moments2_ready, 1)

        def residual(pool, g, par):
            if not ok(g):
                return
            wait(pool, rden_in, 16 * g + 16)
            pool.tensor_tensor(att[:, par], att[:, par], rden[:, par], ALU.mult).then_inc(ratio_done, 1)
            wait(pool, ratio_done, g + 1)
            wait(pool, xres_in, 16 * g + 16)
            pool.tensor_tensor(att[:, par], att[:, par], xres[:, par], ALU.add).then_inc(x2_done, 1)

        def ln2(pool, g):
            if not ok(g):
                return
            steps = [0]

            def step(ins):
                steps[0] += 1
                ins.then_inc(ln2_step, 1)
                wait(pool, ln2_step, LN2_STEPS * g + steps[0])
                settle(pool)

            wait(pool, moments2_ready, g + 1)
            wait(pool, y_done, g)
            settle(pool)
            c = [sm2[:, k:k + 1] for k in range(12)]
            step(pool.tensor_scalar(c[0], mv2[:, 1:2], LN_EPS, None, ALU.add))
            step(pool.tensor_tensor(c[1], c[0], halves[:, 0:1], ALU.pow))
            step(pool.tensor_tensor(c[2], c[0], halves[:, 1:2], ALU.pow))
            step(pool.tensor_tensor(c[3], c[1], c[1], ALU.mult))
            step(pool.tensor_tensor(c[3], c[3], mv2[:, 1:2], ALU.mult))
            step(pool.tensor_scalar(c[3], c[3], RMS_EPS, None, ALU.add))
            step(pool.tensor_tensor(c[4], c[3], halves[:, 0:1], ALU.pow))
            step(pool.tensor_tensor(c[5], c[3], halves[:, 1:2], ALU.pow))
            step(pool.tensor_tensor(c[6], c[1], c[4], ALU.mult))
            step(pool.tensor_tensor(c[8], c[6], mv2[:, 0:1], ALU.mult))
            step(pool.tensor_scalar(c[7], c[8], -1.0, None, ALU.mult))
            wait(pool, y_out, 16 * g)
            settle(pool)
            step(pool.tensor_scalar(ytile[:, L:L + 1], c[2], 1.0, c[5], ALU.add, ALU.mult))
            step(pool.tensor_copy(ytile[:, L + 1:L + 2], mv2[:, 0:1]))

        attention = ExitStack()
        block = attention.enter_context(nc.Block())

        @block.sync
        def _(sp):
            def load_in(g):
                if not ok(g):
                    return
                wait(sp, parts_ready, 2 * g)
                sp.dma_start(xin, x[bass.ds(g, 1)].rearrange("a p q -> (a p) q")).then_inc(xk_in, 16)
                sp.dma_start(kin, ctx_k[bass.ds(g, 1)].rearrange("a p q -> (a p) q")).then_inc(xk_in, 16)

            def put_parts(g):
                if not ok(g):
                    return
                wait(sp, parts_ready, 2 * (g + 1))
                sp.dma_start(split_d[bass.ds(g, 1)].rearrange("a p s q -> (a p) s q"), parts)\
                    .then_inc(split_out, 16)

            def load_stacks(g, par):
                if not ok(g):
                    return
                counts = [16 * (g + 1), 8 * (g - 1)]
                if not isinstance(g, int):
                    counts = [sp.snap(c) for c in counts]
                wait(sp, split_out, counts[0])
                settle(sp)
                wait(sp, st_done, counts[1])
                src = split_d[bass.ds(g, 1)].rearrange("a (j d) s q -> d (a j) s q", j=GH)
                for r, (sq, sk) in enumerate(((0, 2), (0, 3), (1, 2))):
                    rows = slice(r * HD, (r + 1) * HD)
                    sp.dma_start(qst[rows, par], src[:, :, sq]).then_inc(stack_in, 16)
                    sp.dma_start(kst[rows, par], src[:, :, sk]).then_inc(stack_in, 16)

            def load_v(g, par):
                if not ok(g):
                    return
                wait(sp, pv_done, 4 * (g - 1))
                for e in range(2):
                    sp.dma_start(
                        vt[:, par, :, :, e * 4 * HD:(e * 4 + 1) * HD].rearrange("p c k n -> p (c k) n"),
                        ctx_v[bass.ds(g, 1), e].rearrange("a p c n -> (a p) c n")).then_inc(v_in, 16)

            def load_res(g, par):
                wait(sp, x2_done, g - 1)
                sp.dma_start(xres[:, par], x[bass.ds(g, 1)].rearrange("a p q -> (a p) q"))\
                    .then_inc(xres_in, 16)

            load_in(0)
            sp.dma_start(klen_i[:, :], bass.AP(klen.tensor, 0, [[0, P], [1, B]])).then_inc(const_in, 16)
            sp.dma_start(ident[:, :], ident_h).then_inc(const_in, 16)
            sp.dma_start(us[0:EXPERTS, :], us_h).then_inc(const_in, 16)
            sp.dma_start(wn[:, :], w_h).then_inc(const_in, 16)
            put_parts(0)
            load_in(1)
            load_stacks(0, 0)
            sp.wait_ge(setup_pool, 1)
            load_v(0, 0)
            put_parts(1)
            load_in(2)
            load_stacks(1, 1)

            def body(i):
                for par in range(2):
                    g = 2 * i + par
                    load_res(g, par)
                    load_v(g + 1, 1 - par)
                    collect_den(sp, g - 1, 1 - par)
                    spread_inverses(sp, g - 1, 1 - par)
                    put_parts(g + 2)
                    load_in(g + 3)
                    put_y(sp, g - 2)
                    load_stacks(g + 2, par)

            bodies(sp, body, last=2)

        @block.tensor
        def _(pe):
            def scores_q(h, half):
                if not h.exists:
                    return
                if h.j == 0 and half == 0:
                    wait(pe, stack_in, 96 * h.g + 96)
                wait(pe, max_done, 2 * h.n + half)
                for t in range(2):
                    q = (2 * half + t) * P
                    mm = pe.matmul(sq_ps[:, t, :], qst[0:96, h.par, h.j, q:q + P],
                                   kst[0:96, h.par, h.j, :], start=True, stop=True)
                mm.then_inc(sq_done, 1)

            def max_rows(h):
                if not h.exists:
                    return
                wait(pe, mneg_done, h.n + 1)
                wait(pe, mrow_copied, h.n)
                for t in range(KC):
                    mm = pe.matmul(mt_ps[96:98, t * P:(t + 1) * P], mhl[:, h.slot, t, :], ident16[:, :],
                                   start=True, stop=True)
                mm.then_inc(mrow_done, 1)

            def scores_k(h, half):
                wait(pe, mrow_copied, h.n + 1)
                wait(pe, exp_done, 2 * h.n - 1 + half)
                for c in (2 * half, 2 * half + 1):
                    mm = pe.matmul(st_ps[:, c, :], kst[0:98, h.par, h.j, c * P:(c + 1) * P],
                                   qst[0:98, h.par, h.j, :], start=True, stop=True)
                mm.then_inc(st_done, 1)

            def values(h, half):
                if not h.exists:
                    return
                if half == 0 and h.j == 0:
                    wait(pe, v_in, 32 * h.g + 32)
                if half == 0 and h.slot == 0:
                    wait(pe, att_evac, h.pair)
                wait(pe, exp_done, 2 * h.n + 1 + half)
                e = h.slot
                for c in (2 * half, 2 * half + 1):
                    mm = pe.matmul(pv_ps[:, :], vt[:, h.par, c, h.j // 2, 3 * HD * e:3 * HD * e + P],
                                   pt[:, h.slot, c, :], start=(e == 0 and c == 0),
                                   stop=(e == 1 and c == KC - 1))
                if half == 1:
                    mm.then_inc(pv_done, 1)

            for off in (0, 1):
                for half in range(2):
                    scores_q(Head(0, off), half)
            pe.wait_ge(consts_ready, 3)
            max_rows(Head(0, 0))

            def body(i):
                for jj in range(2 * GH):
                    scores_k(Head(i, jj), 0)
                    scores_q(Head(i, jj + 2), 0)
                    scores_k(Head(i, jj), 1)
                    max_rows(Head(i, jj + 1))
                    values(Head(i, jj - 1), 0)
                    scores_q(Head(i, jj + 2), 1)
                    values(Head(i, jj - 1), 1)

            bodies(pe, body)
            values(Head(B - 1, 7), 0)
            values(Head(B - 1, 7), 1)

        @block.scalar
        def _(act):
            def load_w(h):
                if not h.exists:
                    return
                wait(act, sign_done, h.n - 1)
                act.dma_start(stage[:, h.slot], (up_h, dn_h)[h.slot][bass.ds(h.pair, 1)]
                              .rearrange("a p n -> (a p) n")).then_inc(w_in[h.slot], 16)

            load_w(Head(0, 0))
            load_w(Head(0, 1))
            act.wait_ge(setup_dve, 1)
            act.activation(lnk[:, :], lnk[:, :], ACT.Ln).then_inc(lnk_ready, 1)

            def norm_q(g):
                if not ok(g):
                    return
                wait(act, ln1_step, LN1_STEPS * g + LN1_STEPS)
                act.activation(xin, xin, ACT.Identity, bias=sml[:, 3:4], scale=sml[:, 2:3])\
                    .then_inc(q_ready, 1)

            def copy_rows(h):
                if not h.exists:
                    return
                wait(act, mrow_done, h.n + 1)
                act.activation(qst[96:98, h.par, h.j, :], mt_ps[96:98, :], ACT.Copy)\
                    .then_inc(mrow_copied, 1)

            def exps(h, half):
                wait(act, st_done, 2 * h.n + 1 + half)
                wait(act, pv_done, h.n - 1)
                settle(act)
                act.activation(pt[:, h.slot, 2 * half:2 * half + 2, :], st_ps[:, 2 * half:2 * half + 2, :],
                               ACT.Exp, scale=expscale[:, bass.ds(h.g, 1)]).then_inc(exp_done, 1)

            def evacuate(h):
                if not h.exists:
                    return
                rows = slice(64 * (h.j // 2), 64 * (h.j // 2) + 64)
                wait(act, pv_done, h.n + 1)
                if h.j == 1:
                    wait(act, y_done, h.g - 1)
                act.activation(rden[rows, h.par], pv_ps[64:128, :], ACT.Copy)
                act.activation(att[rows, h.par], pv_ps[0:64, :], ACT.Copy).then_inc(att_evac, 1)

            def signs(h):
                wait(act, w_in[h.slot], 16 * h.pair + 16)
                dst = (w_up[:, :, :, :].rearrange("p c e h -> p (c e h)"),
                       w_dn[:, :, :].rearrange("p e n -> p (e n)"))[h.slot]
                act.activation(dst[:, bass.ds(h.pair * CH, CH)], stage[:, h.slot], ACT.Sign)\
                    .then_inc(sign_done, 1)

            norm_q(0)
            norm_q(1)
            copy_rows(Head(0, 0))

            def body(i):
                for jj in range(2 * GH):
                    h = Head(i, jj)
                    exps(h, 0)
                    copy_rows(Head(i, jj + 1))
                    exps(h, 1)
                    signs(h)
                    if h.slot == 0:
                        evacuate(Head(i, jj - 1))
                    if h.j == 1:
                        norm_q(h.g + 2)
                        norm_y(act, h.g - 2, h.par)
                    load_w(Head(i, jj + 2))

            bodies(act, body)
            evacuate(Head(B - 1, 7))

        @block.vector
        def _(dve):
            def prep_stats(g):
                if not ok(g):
                    return
                wait(dve, xk_in, 32 * g + 32)
                dve.bn_stats(stat[:, :], xin).then_inc(stats_ready, 1)
                wait(dve, kpow_step, 4 * g)
                dve.tensor_reduce(small[:, 0:1], kin, AX.X, ALU.max, apply_absolute_value=True)\
                    .then_inc(kmax_ready, 1)
                wait(dve, stats_ready, g + 1)
                wait(dve, q_ready, g)
                settle(dve)
                dve.bn_aggr(mv[:, :], stat[:, :]).then_inc(moments_ready, 1)

            def prep_kpow(g, b):
                if not ok(g):
                    return
                wait(dve, kmax_all, g + 1)
                dve.tensor_scalar(kpow[:, 0:1], small[:, 1:2], 2.0 ** -60, None, ALU.max)\
                    .then_inc(kpow_step, 1)
                wait(dve, kpow_step, 4 * g + 1)
                dve.tensor_scalar(kpow[:, 1:2].bitcast(I32), kpow[:, 0:1].bitcast(I32), EXPO, None,
                                  ALU.bitwise_and).then_inc(kpow_step, 1)
                wait(dve, kpow_step, 4 * g + 2)
                dve.tensor_scalar(kpow[:, 2:3].bitcast(I32), kpow[:, 1:2].bitcast(I32), -1.0,
                                  float(0x7F000000 + (12 << 23)), ALU.mult, ALU.add)\
                    .then_inc(kpow_step, 1)
                wait(dve, setup_dve, 2)
                dve.tensor_tensor(expscale[:, bass.ds(g, 1)], kpow[:, 1:2], lnk[:, bass.ds(b, 1)],
                                  ALU.mult).then_inc(kpow_step, 1)

            def prep_k(g):
                if not ok(g):
                    return
                wait(dve, kpow_step, 4 * g + 3)
                wait(dve, split_out, 16 * g)
                dve.tensor_scalar(parts[:, 2], kin, kpow[:, 2:3], None, ALU.mult).then_inc(hi_ready, 1)
                wait(dve, hi_ready, 2 * g + 1)
                dve.scalar_tensor_tensor(parts[:, 3], kin, kpow[:, 2:3], parts[:, 2], ALU.mult,
                                         ALU.subtract).then_inc(parts_ready, 1)

            def prep_q(g):
                if not ok(g):
                    return
                wait(dve, q_ready, g + 1)
                dve.tensor_copy(parts[:, 0], xin).then_inc(hi_ready, 1)
                wait(dve, hi_ready, 2 * g + 2)
                dve.tensor_tensor(parts[:, 1], xin, parts[:, 0], ALU.subtract).then_inc(parts_ready, 1)

            def reduce_scores(h, half):
                if not h.exists:
                    return
                if half == 0:
                    wait(dve, mneg_done, h.n - 1)
                wait(dve, sq_done, 2 * h.n + half + 1)
                dve.tensor_reduce(mx[:, h.slot, 2 * half:2 * half + 2], sq_ps[:, :, :], AX.X,
                                  ALU.max, negate=True).then_inc(max_done, 1)

            def split_maxima(h):
                if not h.exists:
                    return
                wait(dve, max_done, 2 * h.n + 2)
                wait(dve, mrow_done, h.n - 1)
                dve.tensor_scalar(mhl[:, h.slot, :, 0], mx[:, h.slot, :], 1.0 / K_SCALE, None, ALU.mult)\
                    .then_inc(mhi_done, 1)
                wait(dve, mhi_done, h.n + 1)
                dve.scalar_tensor_tensor(mhl[:, h.slot, :, 1], mx[:, h.slot, :], 1.0 / K_SCALE,
                                         mhl[:, h.slot, :, 0], ALU.mult, ALU.subtract)\
                    .then_inc(mneg_done, 1)

            def sum_signs(h):
                if not h.exists:
                    return
                k = h.pair
                wait(dve, sign_done, 2 * k + 1)
                src = w_up[:, :, :, :].rearrange("p c e h -> p (c e h)")
                dve.tensor_reduce(sums_h[:, bass.ds(8 * k, 8)],
                                  src[:, bass.ds(k * CH, CH)].rearrange("p (e h) -> p e h", h=HID),
                                  AX.X, ALU.add).then_inc(sums_done, 1)

            prep_stats(0)
            dve.wait_ge(const_in, 64)
            dve.tensor_copy(lnk[:, :], klen_i[:, :]).then_inc(setup_dve, 1)
            dve.tensor_copy(ident16[:, :], ident[:, :]).then_inc(consts_ready, 1)
            dve.wait_ge(lnk_ready, 1)
            dve.tensor_scalar(lnk[:, :], lnk[:, :], ATT_SCALE / (Q_SCALE * K_SCALE), None, ALU.mult)\
                .then_inc(setup_dve, 1)
            for g in range(2):
                if g == 1:
                    prep_stats(1)
                prep_kpow(g, 0)
                prep_k(g)
                prep_q(g)
                if g == 0:
                    for par in range(2):
                        dve.memset(kst[96:98, par, :, :], K_SCALE).then_inc(consts_ready, 1)
            n = [0]

            def setup_step(ins):
                n[0] += 1
                ins.then_inc(setup_steps, 1)
                dve.wait_ge(setup_steps, n[0])

            dve.tensor_reduce(mags[:, 0:1], wn[:, :], AX.X, ALU.max, apply_absolute_value=True)\
                .then_inc(mags_ready, 1)
            setup_step(dve.memset(mags[:, 1:2], 0.0))
            dve.tensor_reduce(mags[0:EXPERTS, 1:2], us[0:EXPERTS], AX.X, ALU.max,
                              apply_absolute_value=True)\
                .then_inc(mags_ready, 1)
            for jj in range(2):
                for half in range(2):
                    reduce_scores(Head(0, jj), half)
                split_maxima(Head(0, jj))
            dve.wait_ge(mags_all, 1)
            setup_step(dve.tensor_scalar(powers[:, 0:2], mags[:, 2:4], 2.0 ** -60, None, ALU.max))
            setup_step(dve.tensor_scalar(powers[:, 2:4].bitcast(I32), powers[:, 0:2].bitcast(I32), EXPO, None,
                                   ALU.bitwise_and))
            setup_step(dve.tensor_scalar(powers[:, 4:6].bitcast(I32), powers[:, 2:4].bitcast(I32), -1.0,
                                   float(0x7F000000), ALU.mult, ALU.add))
            setup_step(dve.tensor_scalar(wn[:, :], wn[:, :], powers[:, 4:5], X_SCALE, ALU.mult, ALU.mult))
            setup_step(dve.tensor_scalar(us[0:EXPERTS], us[0:EXPERTS], powers[0:EXPERTS, 5:6], H_SCALE / X_SCALE,
                                   ALU.mult, ALU.mult))
            setup_step(dve.tensor_scalar(powers[:, 0:1], powers[:, 2:3], powers[:, 3:4], 1.0 / H_SCALE,
                                   ALU.mult, ALU.mult))

            def body(i):
                for jj in range(2 * GH):
                    h = Head(i, jj)
                    reduce_scores(Head(i, jj + 2), 0)
                    if h.j == 0:
                        prep_stats(h.g + 2)
                    if h.j == 1:
                        prep_kpow(h.g + 2, i + 1)
                        prep_k(h.g + 2)
                    if h.j == 2:
                        invert(dve, h.g - 1)
                    reduce_scores(Head(i, jj + 2), 1)
                    split_maxima(Head(i, jj + 2))
                    if h.j == 0:
                        stats2(dve, h.g - 2, h.par)
                    if h.j == 2:
                        prep_q(h.g + 2)
                        sum_signs(Head(i, jj - 4))
                    if h.j == 3:
                        sum_signs(Head(i, jj - 3))

            bodies(dve, body, first=2)
            sum_signs(Head(B - 1, 6))

        @block.gpsimd
        def _(pool):
            pool.memset(vt[:, :, :, :, HD:2 * HD], 0.0)
            pool.memset(vt[:, :, :, :, 3 * HD:4 * HD], 0.0)
            pool.memset(vt[:, :, :, :, 5 * HD:6 * HD], 0.0)
            pool.memset(vt[:, :, :, :, 2 * HD:3 * HD], 1.0)
            pool.memset(halves[:, 0:1], -0.5)
            pool.memset(halves[:, 1:2], 0.5)
            pool.memset(ytile[:, L + 2:YROW], 0.0)
            pool.memset(vt[:, :, :, :, 6 * HD:7 * HD], 1.0).then_inc(setup_pool, 1)
            pool.wait_ge(setup_pool, 1)

            def ln1(g):
                if not ok(g):
                    return
                s = LN1_STEPS * g
                wait(pool, kmax_ready, g + 1)
                settle(pool)
                pool.partition_all_reduce(small[:, 1:2], small[:, 0:1], P, ABSMAX).then_inc(kmax_all, 1)
                wait(pool, moments_ready, g + 1)
                settle(pool)
                pool.tensor_scalar(sml[:, 0:1], mv[:, 1:2], LN_EPS, None, ALU.add).then_inc(ln1_step, 1)
                wait(pool, ln1_step, s + 1)
                pool.tensor_tensor(sml[:, 1:2], sml[:, 0:1], halves[:, 0:1], ALU.pow).then_inc(ln1_step, 1)
                wait(pool, ln1_step, s + 2)
                settle(pool)
                pool.tensor_scalar(sml[:, 2:3], sml[:, 1:2], Q_SCALE, None, ALU.mult).then_inc(ln1_step, 1)
                wait(pool, ln1_step, s + 3)
                pool.tensor_tensor(sml[:, 4:5], mv[:, 0:1], sml[:, 2:3], ALU.mult).then_inc(ln1_step, 1)
                wait(pool, ln1_step, s + 4)
                settle(pool)
                pool.tensor_scalar(sml[:, 3:4], sml[:, 4:5], -1.0, None, ALU.mult).then_inc(ln1_step, 1)

            ln1(0)
            ln1(1)
            pool.wait_ge(mags_ready, 2)
            pool.partition_all_reduce(mags[:, 2:4], mags[:, 0:2], P, ABSMAX).then_inc(mags_all, 1)

            def body(i):
                for par in range(2):
                    g = 2 * i + par
                    ln1(g + 2)
                    ln2(pool, g - 2)
                    residual(pool, g - 1, 1 - par)

            bodies(pool, body, first=2)

        attention.close()
        block = stack.enter_context(nc.Block())

        def passes(eng, body, n, first=1, last=1):
            for i in range(first):
                body(i)
            with eng.Fori(first, n - last) as i:
                body(i)
            for i in range(n - last, n):
                body(i)

        class Tile:

            def __init__(self, i, jj, count=TILES, per_pass=4):
                self.n, self.par, self.slot = per_pass * i + jj, jj % 2, jj % per_pass
                self.turn = per_pass // 2 * i + jj // 2
                self.slot_turn = i + jj // per_pass
                self.exists = not isinstance(i, int) or 0 <= self.n < count

        def registers(eng, name):
            return [[eng.alloc_register(f"{name}{k}{b}") for b in range(TB)] for k in range(4)]

        def load_experts(eng, regs, tile):
            settle(eng)
            eng.load(regs[tile.slot], expert_of[0:1, bass.ds(TB * tile.n, TB)])

        def expert(eng, regs, tile, b):
            return eng.snap(regs[tile.slot][b], min_val=0, max_val=EXPERTS - 1)

        def diagonal(par, k):
            return hz[:, par, k].rearrange("p (b n) -> p b n", n=P + BLK)[:, :, 0:BLK]

        @block.sync
        def _(sp):
            sp_regs = registers(sp, "sp_expert")

            def load_rows(tile):
                g = tile.n
                wait(sp, y_out, 16 * g + 16)
                settle(sp)
                wait(sp, tok_t, g - 3)
                sp.dma_start(rows[:, tile.slot], ytab[bass.ds(g, 1)].rearrange("a p q -> (a p) q"))\
                    .then_inc(row_in[tile.slot], 16)

            def load_scales(tile):
                t, par = tile.n, tile.par
                wait(sp, prod_ready, t - 1)
                load_experts(sp, sp_regs, tile)
                for b in range(TB):
                    e = expert(sp, sp_regs, tile, b)
                    sp.dma_start(scl[b * BLK:(b + 1) * BLK, par],
                                 sctab[bass.ds(e, 1), :].broadcast_to([BLK, L])).then_inc(scl_in[par], 16)

            def body_rows(i):
                for k in range(4):
                    load_rows(Tile(i, k))

            def body_scales(i):
                for k in range(4):
                    load_scales(Tile(i, k))

            collect_den(sp, GROUPS - 1, 1)
            body_rows(0)
            sp.dma_start(cst, cst_h).then_inc(cst_in, 16)
            sp.dma_start(ds_sb[0:EXPERTS], ds_h).then_inc(scale_in, 16)
            sp.dma_start(os_sb[0:EXPERTS], os_h).then_inc(scale_in, 16)
            spread_inverses(sp, GROUPS - 1, 1)
            with sp.Fori(1, GROUPS // 4 - 1) as i:
                body_rows(i)
            put_y(sp, GROUPS - 2)
            for k in range(3):
                load_rows(Tile(GROUPS // 4 - 1, k))
            put_y(sp, GROUPS - 1)
            sp.wait_ge(sctab_ready, 1)
            sp.dma_start(sctab, scale_sb[0:EXPERTS]).then_inc(sctab_out, 16)
            sp.wait_ge(sctab_out, 16)
            sp.wait_ge(expert_ready, 1)
            passes(sp, body_scales, TILES // 4)

        @block.tensor
        def _(pe):
            t_ps = [st_ps[:, k, :].rearrange("p (c n) -> p c n", c=KC) for k in range(2)]
            h_ps = [st_ps[:, k, 0:2 * P].rearrange("p (b k n) -> p b k n", b=TB, k=2) for k in (2, 3)]
            pe_regs = registers(pe, "pe_expert")

            def turn_rows(tile):
                if not tile.exists:
                    return
                g, par = tile.n, tile.par
                last = isinstance(g, int) and g == GROUPS - 1
                if last:
                    pe.wait_ge(y_done, GROUPS)
                else:
                    wait(pe, row_in[tile.slot], 16 * tile.slot_turn + 16)
                src = ytile if last else rows[:, tile.slot]
                wait(pe, xt_ready, g - 1)
                for c in range(KC):
                    mm = pe.transpose(t_ps[par][:, c, :], src[:, c * P:(c + 1) * P], ident[:, :])
                mm.then_inc(tok_t, 1)

            def scores(tile):
                g, par = tile.n, tile.par
                wait(pe, xt_ready, g + 1)
                wait(pe, score_copied, g - 3)
                for c in range(KC):
                    mm = pe.matmul(banks[tile.slot][:, 0:EXPERTS + CLUSTERS], xt[:, par, c], sigw[:, c],
                                   start=(c == 0), stop=(c == KC - 1))
                mm.then_inc(score_done, 1)

            def body_scores(i):
                for k in range(4):
                    turn_rows(Tile(i, k + 1, GROUPS))
                    if k == 0 and isinstance(i, int) and i == 0:
                        pe.wait_ge(sig_ready, 1)
                    scores(Tile(i, k, GROUPS))

            turn_rows(Tile(0, 0, GROUPS))
            passes(pe, body_scores, GROUPS // 4)

            flat = onehot[:, :, :].rearrange("p g e -> p (g e)")
            half_tiles = GROUPS // 2
            pe.wait_ge(xt_ready, GROUPS)
            pe.wait_ge(score_copied, GROUPS)
            for half in range(2):
                pe.wait_ge(onehot_ready, GROUPS // 4 // 2 * (half + 1))
                for g in range(half_tiles * half, half_tiles * (half + 1)):
                    mm = pe.matmul(banks[2][0:EXPERTS, 0:P], onehot[:, g, :], ones16,
                                   start=(g == 0), stop=(g == GROUPS - 1))
                if half == 1:
                    mm.then_inc(count_done, 1)
                pe.matmul(st_ps[:, half, :], tri16, flat[:, half * L:(half + 1) * L],
                          start=True, stop=False)
                if half == 1:
                    pe.matmul(st_ps[:, half, :], ones16,
                              early.unsqueeze(1).to_broadcast([P, half_tiles, EXPERTS]),
                              start=False, stop=False)
                for k in range(half_tiles - 1):
                    g = half * half_tiles + k
                    pe.matmul(st_ps[:, half, (k + 1) * EXPERTS:], ones16,
                              onehot[:, g:g + 1, :].to_broadcast([P, half_tiles - 1 - k, EXPERTS]),
                              start=False, stop=False)
            pe.wait_ge(nblk_ready, 1)
            for half in range(2):
                mm = pe.matmul(st_ps[:, half, :], nblk[0:EXPERTS],
                               tri_blk[0:EXPERTS].unsqueeze(1).to_broadcast([EXPERTS, half_tiles, EXPERTS]),
                               start=False, stop=True)
            mm.then_inc(rank_done, 1)
            pe.matmul(banks[1][0:EXPERTS, 0:P], tri16[0:EXPERTS, 0:EXPERTS], nblk[0:EXPERTS],
                      start=True, stop=True).then_inc(start_done, 1)
            pe.wait_ge(slots_ready, 1)
            pe.wait_ge(numbered, 1)
            for g in range(GROUPS):
                mm = pe.matmul(banks[2][:, 0:TILES], slot_p[:, g], slot_a[:, g],
                               start=(g == 0), stop=(g == GROUPS - 1))
            mm.then_inc(list_done, 1)
            pe.wait_ge(ended_ready, 1)
            pe.matmul(banks[3][:, 0:BLOCKS], ones16[0:EXPERTS], ended[0:EXPERTS],
                      start=True, stop=True).then_inc(expert_done, 1)
            pe.wait_ge(live_ready, 1)
            pe.matmul(banks[1][:, 0:BLOCKS], us[0:EXPERTS], live[0:EXPERTS],
                      start=True, stop=True).then_inc(us_done, 1)

            def turn_slots(tile):
                if not tile.exists:
                    return
                t, par = tile.n, tile.par
                wait(pe, gathered[tile.slot], 16 * tile.slot_turn + 16)
                wait(pe, xlo_ready, t - 1)
                for c in range(KC):
                    mm = pe.transpose(t_ps[par][:, c, :], rows[:, tile.slot, c * P:(c + 1) * P], ident[:, :])
                mm.then_inc(slot_t, 1)

            def up(tile, b):
                e = expert(pe, pe_regs, tile, b)
                cols = slice(b * BLK, (b + 1) * BLK)
                for c in range(KC):
                    w = w_up[:, c, bass.ds(e, 1), :].rearrange("p a h -> p (a h)")
                    mm = pe.matmul(h_ps[tile.par][:, b], w, xhl[:, tile.par, :, c, cols],
                                   start=(c == 0), stop=(c == KC - 1))
                if b == TB - 1:
                    mm.then_inc(up_done, 1)

            def down(tile, b):
                if not tile.exists:
                    return
                e = expert(pe, pe_regs, tile, b)
                w = w_dn[:, bass.ds(e, 1), :].rearrange("p a n -> p (a n)")
                for k in range(2):
                    mm = pe.matmul(banks[tile.par], hz[:, tile.par, k, b * P:(b + 1) * P], w,
                                   start=(b == 0 and k == 0), stop=(b == TB - 1 and k == 1))
                if b == TB - 1:
                    mm.then_inc(down_done, 1)

            def await_up(tile):
                wait(pe, xlo_ready, tile.n + 1)
                wait(pe, hid_ready, tile.n - 1)

            def await_down(tile):
                if not tile.exists:
                    return
                wait(pe, hlo_ready, tile.n + 1)
                wait(pe, prod_ready, tile.n - 1)

            def body_slots(i):
                for k in range(4):
                    turn_slots(Tile(i, k + 1))
                    if Tile(i, k + 1).exists:
                        load_experts(pe, pe_regs, Tile(i, k + 1))
                    await_up(Tile(i, k))
                    for b in range(TB):
                        up(Tile(i, k), b)
                        if b == 0:
                            await_down(Tile(i, k - 2))
                        down(Tile(i, k - 2), b)

            pe.wait_ge(expert_ready, 1)
            load_experts(pe, pe_regs, Tile(0, 0))
            turn_slots(Tile(0, 0))
            passes(pe, body_slots, TILES // 4)
            for k in (2, 3):
                await_down(Tile(TILES // 4 - 1, k))
                for b in range(TB):
                    down(Tile(TILES // 4 - 1, k), b)

        @block.scalar
        def _(act):
            sums = sums_h[:, :].rearrange("p (c e) -> p c e", c=KC)
            act.activation(sigw[:, :, 0:EXPERTS], sums, ACT.Sign).then_inc(sig_tiles, 1)
            act.wait_ge(csum_ready, 1)
            act.activation(sigw[:, :, EXPERTS:], csum[:, :, :], ACT.Sign).then_inc(sig_clusters, 1)

            def copy_xt(tile):
                if not tile.exists:
                    return
                g, par = tile.n, tile.par
                wait(act, tok_t, g + 1)
                wait(act, score_done, g - 1)
                act.activation(xt[:, par].rearrange("p c n -> p (c n)"), st_ps[:, par, :], ACT.Copy)\
                    .then_inc(xt_ready, 1)

            def body_rows(i):
                for k in range(4):
                    copy_xt(Tile(i, k, GROUPS))

            body_rows(0)
            norm_y(act, GROUPS - 2, 0)
            body_rows(1)
            for k in range(4):
                copy_xt(Tile(2, k))
                if k == 3:
                    norm_y(act, GROUPS - 1, 1)
            body_rows(3)

            def split_high(tile):
                if not tile.exists:
                    return
                t, par = tile.n, tile.par
                wait(act, slot_t, t + 1)
                wait(act, up_done, t - 1)
                for c in range(KC):
                    ins = act.activation(xhl[:, par, 0, c], st_ps[:, par, c * P:(c + 1) * P], ACT.Copy,
                                         scale=wn[:, c:c + 1])
                ins.then_inc(xhi_ready, 1)

            def hidden_high(tile):
                t, par = tile.n, tile.par
                wait(act, hsum_ready, t + 1)
                wait(act, down_done, t - 1)
                act.activation(diagonal(par, 0), hid[:, par], ACT.Relu).then_inc(hhi_ready, 1)

            def residual(tile):
                if not tile.exists:
                    return
                t, par = tile.n, tile.par
                wait(act, gathered[tile.slot], 16 * tile.slot_turn + 16)
                wait(act, res_ready, t - 1)
                act.activation(base[:, par], rows[:, tile.slot, 0:L], ACT.Identity,
                               bias=rows[:, tile.slot, L + 1:L + 2], scale=rows[:, tile.slot, L:L + 1])\
                    .then_inc(base_ready, 1)

            def body_slots(i):
                for k in range(4):
                    split_high(Tile(i, k + 1))
                    residual(Tile(i, k - 1))
                    hidden_high(Tile(i, k))

            act.wait_ge(clean, 2)
            split_high(Tile(0, 0))
            passes(act, body_slots, TILES // 4)
            residual(Tile(TILES // 4 - 1, 3))

        @block.vector
        def _(dve):
            n = [0]

            def step(ins):
                n[0] += 1
                ins.then_inc(ffn_step, 1)
                dve.wait_ge(ffn_step, n[0])

            stats2(dve, GROUPS - 2, 0)
            sigs = sigw[:, :, :]
            dve.wait_ge(sig_tiles, 1)
            dve.tensor_reduce(csum[:, :, :], sigs[:, :, 0:EXPERTS].rearrange(
                "p c (a b) -> p c a b", b=EXPERTS // CLUSTERS), AX.X, ALU.add).then_inc(csum_ready, 1)
            dve.wait_ge(sig_clusters, 1)
            dve.tensor_tensor(sigs, sigs, wn[:, :].unsqueeze(2).to_broadcast(
                [P, KC, EXPERTS + CLUSTERS]), ALU.mult).then_inc(sig_ready, 1)
            invert(dve, GROUPS - 1)
            dve.wait_ge(scale_in, 32)
            dve.tensor_scalar(scale_sb[0:EXPERTS], ds_sb[0:EXPERTS], os_sb[0:EXPERTS, 0:1],
                              powers[0:EXPERTS, 0:1], ALU.mult, ALU.mult).then_inc(sctab_ready, 1)
            dve.wait_ge(cst_in, 16)
            dve.tensor_copy(tri16, cst[:, C_TRI:C_TRI + P])
            dve.tensor_scalar(tri_blk, cst[:, C_TRI:C_TRI + EXPERTS], float(BLK), None, ALU.mult)
            dve.memset(ones16, 1.0)

            def copy_scores(tile):
                g = tile.n
                wait(dve, score_done, g + 1)
                dve.tensor_copy(score[:, tile.slot], banks[tile.slot][:, 0:EXPERTS + CLUSTERS])\
                    .then_inc(score_copied, 1)

            def per_tile(col, width, tiles=GROUPS):
                return col.unsqueeze(2).to_broadcast([P, tiles, width])

            def per_expert(c0, width, tiles=GROUPS):
                return cst[:, c0:c0 + width].unsqueeze(1).to_broadcast([P, tiles, width])

            top, first, ttop, expert_no = pick

            def route(i):
                done = [0]

                def route_step(ins):
                    done[0] += 1
                    ins.then_inc(routed, 1)
                    wait(dve, routed, 10 * i + done[0])

                a, b = near[:, 0], near[:, 1]
                tiles_s, clusters_s = score[:, :, 0:EXPERTS], score[:, :, EXPERTS:]
                wait(dve, score_copied, 4 * i + 4)
                route_step(dve.tensor_reduce(top, clusters_s, AX.X, ALU.max))
                route_step(dve.tensor_tensor(ckey, clusters_s, per_tile(top, CLUSTERS, 4), ALU.is_lt))
                route_step(dve.scalar_tensor_tensor(ckey, ckey, 64.0, per_expert(C_CL8, CLUSTERS, 4),
                                                    ALU.mult, ALU.add))
                route_step(dve.tensor_reduce(first, ckey, AX.X, ALU.min))
                route_step(dve.tensor_tensor(a, per_expert(C_CL64, EXPERTS, 4),
                                             per_tile(first, EXPERTS, 4), ALU.not_equal))
                route_step(dve.scalar_tensor_tensor(b, a, -3e38, tiles_s, ALU.mult, ALU.add))
                route_step(dve.tensor_reduce(ttop, b, AX.X, ALU.max))
                route_step(dve.tensor_tensor(a, b, per_tile(ttop, EXPERTS, 4), ALU.is_lt))
                route_step(dve.scalar_tensor_tensor(b, a, 128.0, per_expert(C_E64, EXPERTS, 4),
                                                    ALU.mult, ALU.add))
                route_step(dve.tensor_reduce(expert_no, b, AX.X, ALU.min))
                dve.tensor_tensor(onehot[:, bass.ds(4 * i, 4), :], per_expert(C_E64, EXPERTS, 4),
                                  per_tile(expert_no, EXPERTS, 4), ALU.is_equal)\
                    .then_inc(onehot_ready, 1)

            def body_scores(i):
                for k in range(4):
                    copy_scores(Tile(i, k))
                route(i)

            body_scores(0)
            stats2(dve, GROUPS - 1, 1)
            body_scores(1)
            dve.wait_ge(onehot_ready, 2)
            step(dve.tensor_reduce(early_f, onehot[:, 0:GROUPS // 2, :].rearrange("p g e -> p e g"),
                                   AX.X, ALU.add))
            step(dve.tensor_copy(early, early_f))
            for i in range(2, GROUPS // 4):
                body_scores(i)

            dve.wait_ge(count_done, 1)
            step(dve.tensor_scalar(counts_i[0:EXPERTS], banks[2][0:EXPERTS, 0:P], float(BLK - 1), None,
                                   ALU.add))
            step(dve.tensor_scalar(counts_i[0:EXPERTS], counts_i[0:EXPERTS], int(math.log2(BLK)), None,
                                   ALU.arith_shift_right))
            dve.tensor_copy(nblk[0:EXPERTS], counts_i[0:EXPERTS]).then_inc(nblk_ready, 1)
            dve.wait_ge(rank_done, 1)
            slots = st_ps[:, 0:2, :].rearrange("p c (g e) -> p (c g) e", e=EXPERTS)
            step(dve.tensor_tensor(mine, slots, onehot, ALU.mult))
            step(dve.tensor_reduce(slot_f, mine, AX.X, ALU.add))
            step(dve.tensor_copy(slot_i[:, 0], slot_f))
            step(dve.tensor_scalar(slot_i[:, 2], slot_i[:, 0], int(math.log2(P)), None,
                                   ALU.arith_shift_right))
            dve.tensor_scalar(slot_i[:, 1], slot_i[:, 0], P - 1, None, ALU.bitwise_and)\
                .then_inc(slot_low, 1)
            dve.tensor_tensor(slot_a, per_expert(C_A32, TILES), per_tile(slot_i[:, 2], TILES),
                              ALU.is_equal).then_inc(slot_high, 1)
            dve.wait_ge(slot_low, 1)
            dve.tensor_tensor(slot_p, per_expert(C_ROWP, P), per_tile(slot_i[:, 1], P), ALU.is_equal)\
                .then_inc(slots_ready, 1)
            dve.wait_ge(start_done, 1)
            dve.wait_ge(nblk_ready, 1)
            step(dve.tensor_tensor(ends[0:EXPERTS], banks[1][0:EXPERTS, 0:P], nblk[0:EXPERTS], ALU.add))
            block_no = cst[0:EXPERTS, C_ROWP:C_ROWP + P]
            step(dve.tensor_tensor(ended[0:EXPERTS], ends[0:EXPERTS], block_no, ALU.is_le))
            dve.tensor_tensor(live[0:EXPERTS], banks[1][0:EXPERTS, 0:P], block_no, ALU.is_le)\
                .then_inc(ended_ready, 1)
            dve.wait_ge(ended_ready, 1)
            dve.tensor_tensor(live[0:EXPERTS], live[0:EXPERTS], ended[0:EXPERTS], ALU.subtract)\
                .then_inc(live_ready, 1)
            dve.wait_ge(list_done, 1)
            step(dve.tensor_scalar(absent, banks[2][:, 0:TILES], 0.5, 1e6, ALU.is_lt, ALU.mult))
            dve.scalar_tensor_tensor(token_of, banks[2][:, 0:TILES], -1.0, absent, ALU.add, ALU.add)\
                .then_inc(list_ready, 1)
            dve.wait_ge(expert_done, 1)
            dve.tensor_scalar(expert_of, banks[3][:, 0:BLOCKS], float(EXPERTS - 1), None, ALU.min)\
                .then_inc(expert_ready, 1)
            dve.wait_ge(us_done, 1)
            step(dve.tensor_copy(us_of, banks[1][:, 0:BLOCKS]))

            def split_low(tile):
                if not tile.exists:
                    return
                t, par = tile.n, tile.par
                wait(dve, xhi_ready, t + 1)
                for c in range(KC):
                    ins = dve.scalar_tensor_tensor(xhl[:, par, 1, c], st_ps[:, par, c * P:(c + 1) * P],
                                                   wn[:, c:c + 1], xhl[:, par, 0, c], ALU.mult,
                                                   ALU.subtract)
                ins.then_inc(xlo_ready, 1)

            def hidden(tile):
                t, par = tile.n, tile.par
                wait(dve, up_done, t + 1)
                wait(dve, hlo_ready, t - 1)
                dve.tensor_tensor(
                    hparts[:, par], st_ps[:, 2 + par, 0:2 * P].rearrange("p (b n) -> p b n", b=TB),
                    us_of[:, bass.ds(TB * t, TB)].unsqueeze(2).to_broadcast([P, TB, 2 * BLK]),
                    ALU.mult).then_inc(hid_ready, 1)
                wait(dve, hid_ready, t + 1)
                dve.tensor_tensor(hid[:, par], hparts[:, par, :, 0:BLK], hparts[:, par, :, BLK:],
                                  ALU.add).then_inc(hsum_ready, 1)

            def hidden_low(tile):
                t, par = tile.n, tile.par
                wait(dve, hhi_ready, t + 1)
                dve.scalar_tensor_tensor(diagonal(par, 1), hid[:, par], 0.0, diagonal(par, 0),
                                         ALU.max, ALU.subtract).then_inc(hlo_ready, 1)

            def scaled(tile):
                if not tile.exists:
                    return
                t, par = tile.n, tile.par
                wait(dve, down_done, t + 1)
                wait(dve, scl_in[par], 16 * TB * (tile.turn + 1))
                wait(dve, scattered[tile.slot], 16 * tile.slot_turn)
                dve.tensor_tensor(res[:, tile.slot], banks[par], scl[:, par], ALU.mult)\
                    .then_inc(prod_ready, 1)
                wait(dve, prod_ready, t + 1)
                wait(dve, base_ready, t + 1)
                dve.tensor_tensor(res[:, tile.slot], res[:, tile.slot], base[:, par], ALU.add)\
                    .then_inc(res_ready, 1)

            def body_slots(i):
                for k in range(4):
                    split_low(Tile(i, k + 1))
                    hidden(Tile(i, k))
                    scaled(Tile(i, k - 2))
                    hidden_low(Tile(i, k))

            dve.wait_ge(expert_ready, 1)
            split_low(Tile(0, 0))
            passes(dve, body_slots, TILES // 4, first=2)
            scaled(Tile(TILES // 4 - 1, 2))
            scaled(Tile(TILES // 4 - 1, 3))

        @block.gpsimd
        def _(pool):
            ln2(pool, GROUPS - 2)
            residual(pool, GROUPS - 1, 1)
            ln2(pool, GROUPS - 1)
            pool.memset(hz[:, 0], 0.0).then_inc(clean, 1)
            pool.memset(hz[:, 1], 0.0).then_inc(clean, 1)
            pool.wait_ge(tok_t, GROUPS)
            pool.wait_ge(y_out, 16 * GROUPS)

            def gather(tile):
                if not tile.exists:
                    return
                t, k = tile.n, tile.slot
                wait(pool, slot_t, t - 3)
                wait(pool, base_ready, t - 3)
                settle(pool)
                pool.tensor_copy(gidx[:, k:k + 1], token_of[:, bass.ds(t, 1)]).then_inc(gidx_ready, 1)
                wait(pool, gidx_ready, t + 1)
                settle(pool)
                pool.indirect_dma_start(
                    rows[:, k], None, ytab.rearrange("g p n -> (g p) n"),
                    bass.IndirectOffsetOnAxis(ap=gidx[:, k:k + 1], axis=0),
                    bounds_check=TOKENS - 1, oob_is_err=False).then_inc(gathered[k], 16)

            def finish(tile):
                if not tile.exists:
                    return
                t, k = tile.n, tile.slot
                wait(pool, scattered[k], 16 * tile.slot_turn)
                settle(pool)
                pool.tensor_copy(sidx[:, k:k + 1], token_of[:, bass.ds(t, 1)]).then_inc(sidx_ready, 1)
                wait(pool, sidx_ready, t + 1)
                wait(pool, res_ready, t + 1)
                settle(pool)
                pool.indirect_dma_start(
                    out, bass.IndirectOffsetOnAxis(ap=sidx[:, k:k + 1], axis=0),
                    res[:, k], None, bounds_check=TOKENS - 1, oob_is_err=False)\
                    .then_inc(scattered[k], 16)

            def body_slots(i):
                for k in range(4):
                    gather(Tile(i, k + 3))
                    finish(Tile(i, k - 2))

            pool.wait_ge(slot_high, 1)
            pool.tensor_tensor(slot_a, slot_a, cst[:, C_TOK:C_TOK + GROUPS].unsqueeze(2).to_broadcast(
                [P, GROUPS, TILES]), ALU.mult).then_inc(numbered, 1)
            pool.wait_ge(list_ready, 1)
            for k in range(3):
                gather(Tile(0, k))
            passes(pool, body_slots, TILES // 4, first=2, last=1)
            finish(Tile(TILES // 4 - 1, 2))
            finish(Tile(TILES // 4 - 1, 3))
            for k in range(4):
                pool.wait_ge(scattered[k], 16 * (TILES // 4))


_INS = ["x", "ctx_k", "ctx_v", "klen", "up_h", "dn_h", "us_h", "ds_h", "os_h", "w_h",
       "ident_h", "cst_h"]


def lay_out(i):
    import numpy as np

    a = {k: np.asarray(v) for k, v in i.items()}
    ctx = a["ctx_2048"]
    up, dn = a["L0_ffn_up_w"], a["L0_ffn_down_w"]
    return {
        "x": a["x"].reshape(GROUPS, P, L),
        "ctx_k": ctx.reshape(GROUPS, P, L),
        "ctx_v": ctx.reshape(GROUPS, 2, 2, HD, KC, P).transpose(0, 2, 5, 4, 1, 3).reshape(
            GROUPS, 2, P, KC * 2, HD),
        "klen": a["itok_B_779_1933"],
        "up_h": up.reshape(8, 8, HID, KC, P).transpose(3, 0, 4, 1, 2).reshape(NUP, P, CH),
        "dn_h": dn.reshape(NUP, 2, L, HID).transpose(0, 3, 1, 2).reshape(NUP, P, CH),
        "us_h": a["L0_ffn_up_scale"],
        "ds_h": a["L0_ffn_down_scale"],
        "os_h": a["L0_ffn_output_scale"].reshape(EXPERTS, 1),
        "w_h": a["L0_ffn_norm_weight"].reshape(KC, P).T,
        "ident_h": np.eye(P, dtype=np.float32),
        "cst_h": constants(),
    }


def kernel(**inputs):
    import numpy as np
    import concourse.bacc as bacc
    from concourse.bass_utils import run_bass_kernel_spmd

    nc = bacc.Bacc("TRN2", target_bir_lowering=False, num_devices=1)
    arrays, args = {}, []
    laid = lay_out(inputs)
    for name in _INS:
        arr = np.ascontiguousarray(laid[name])
        arrays[f"in_{name}"] = arr
        args.append(nc.dram_tensor(f"in_{name}", arr.shape, mybir.dt.from_np(arr.dtype),
                                   kind="ExternalInput").ap())
    out = nc.dram_tensor("out_0", (TOKENS, L), F32, kind="ExternalOutput").ap()
    split_d = nc.dram_tensor("split_d", (GROUPS, P, 4, L), F16, kind="Internal").ap()
    inv_d = nc.dram_tensor("inv_d", (GH, L), F32, kind="Internal").ap()
    ytab = nc.dram_tensor("ytab", (GROUPS, P, YROW), F32, kind="Internal").ap()
    sctab = nc.dram_tensor("sctab", (EXPERTS, L), F32, kind="Internal").ap()
    build(nc, *args, out, split_d, inv_d, ytab, sctab)
    res = run_bass_kernel_spmd(nc, [arrays], core_ids=[0])
    return res.results[0]["out_0"].reshape(B, C, L)
```
